# Optimizing a Trainium2 kernel written in Bass

```python
import numpy as np
import jax
import jax.numpy as jnp

def _softmax(x, axis=-1):
    return jax.nn.softmax(x, axis=axis)

def _gelu(x):
    return jax.nn.gelu(x, approximate=True)

def _silu(x):
    return jax.nn.silu(x)

def _sigmoid(x):
    return jax.nn.sigmoid(x)

def _layernorm(x, axis=-1, eps=1e-05):
    m = jnp.mean(x, axis=axis, keepdims=True)
    v = jnp.var(x, axis=axis, keepdims=True)
    return (x - m) / jnp.sqrt(v + eps)

def _scatter_add(tgt, idx, src, axis=0):
    return tgt.at[idx].add(src)

def _segment_sum(src, seg, n):
    return jax.ops.segment_sum(src, seg, n)
kernel_name = 'mk_seq_postln_d1_jaxref_r4_10acc4'

def setup_inputs(seed: int=0):
    np.random.seed(seed)
    _w = jnp.asarray

    def _L0_attn_setup():
        import jax, jax.numpy as jnp
        import numpy as np
        D_MODEL = 256
        D_STATE = 16
        D_CONV = 4
        EXPAND = 2
        D_INNER = EXPAND * D_MODEL
        DT_RANK = D_MODEL // 16
        BATCH = 4
        SEQ = 512
        key = jax.random.key(seed)
        ks = jax.random.split(key, 9)
        s = lambda k, shape, sc: jax.random.normal(k, shape, jnp.float32) * sc
        x = s(ks[0], (BATCH, SEQ, D_MODEL), 1.0)
        W_in = s(ks[1], (2 * D_INNER, D_MODEL), D_MODEL ** (-0.5))
        conv_w = s(ks[2], (D_INNER, D_CONV), D_CONV ** (-0.5))
        conv_b = s(ks[3], (D_INNER,), 0.02)
        W_xproj = s(ks[4], (DT_RANK + 2 * D_STATE, D_INNER), D_INNER ** (-0.5))
        W_dt = s(ks[5], (D_INNER, DT_RANK), DT_RANK ** (-0.5))
        b_dt = jax.random.uniform(ks[6], (D_INNER,), jnp.float32, -4.0, -1.0)
        A_log = jnp.log(jnp.tile(jnp.arange(1, D_STATE + 1, dtype=jnp.float32), (D_INNER, 1)))
        D_skip = jnp.ones((D_INNER,), jnp.float32)
        W_out = s(ks[7], (D_MODEL, D_INNER), D_INNER ** (-0.5))
        return dict(x=x, W_in=W_in, conv_w=conv_w, conv_b=conv_b, W_xproj=W_xproj, W_dt=W_dt, b_dt=b_dt, A_log=A_log, D_skip=D_skip, W_out=W_out)
    _L0_attn_in = _L0_attn_setup()

    def _L0_ffn_setup():
        import jax, jax.numpy as jnp
        import numpy as np
        DIM = 256
        HIDDEN = 768
        SCALE = 1.0 / 127.0

        def _dequant(w_int, dtype):
            return w_int.astype(dtype) * jnp.asarray(SCALE, dtype)
        key = jax.random.key(seed)
        k_x, k_g, k_u, k_d = jax.random.split(key, 4)
        x = jax.random.normal(k_x, (4, 512, DIM), dtype=jnp.float32)
        w_gate = jax.random.randint(k_g, (HIDDEN, DIM), -127, 128, dtype=jnp.int32)
        w_up = jax.random.randint(k_u, (HIDDEN, DIM), -127, 128, dtype=jnp.int32)
        w_down = jax.random.randint(k_d, (DIM, HIDDEN), -127, 128, dtype=jnp.int32)
        return {'x': x, 'w_gate': w_gate, 'w_up': w_up, 'w_down': w_down}
    _L0_ffn_in = _L0_ffn_setup()
    _d = {'L0_attn_x': _L0_attn_in['x'], 'L0_attn_W_in': _L0_attn_in['W_in'], 'L0_attn_conv_w': _L0_attn_in['conv_w'], 'L0_attn_conv_b': _L0_attn_in['conv_b'], 'L0_attn_W_xproj': _L0_attn_in['W_xproj'], 'L0_attn_W_dt': _L0_attn_in['W_dt'], 'L0_attn_b_dt': _L0_attn_in['b_dt'], 'L0_attn_A_log': _L0_attn_in['A_log'], 'L0_attn_D_skip': _L0_attn_in['D_skip'], 'L0_attn_W_out': _L0_attn_in['W_out'], 'L0_ffn_w_gate': _L0_ffn_in['w_gate'], 'L0_ffn_w_up': _L0_ffn_in['w_up'], 'L0_ffn_w_down': _L0_ffn_in['w_down']}
    _x0 = _d['L0_attn_x']
    _d['L0_attn_x'] = jax.random.normal(jax.random.fold_in(jax.random.key(seed), 1), (8, 1024, 256), dtype=_x0.dtype)
    del _x0
    return _d

def reference(L0_attn_x, L0_attn_W_in, L0_attn_conv_w, L0_attn_conv_b, L0_attn_W_xproj, L0_attn_W_dt, L0_attn_b_dt, L0_attn_A_log, L0_attn_D_skip, L0_attn_W_out, L0_ffn_w_gate, L0_ffn_w_up, L0_ffn_w_down):

    def _L0_attn_ref(x, W_in, conv_w, conv_b, W_xproj, W_dt, b_dt, A_log, D_skip, W_out):
        import jax, jax.numpy as jnp
        import numpy as np
        D_MODEL = 256
        D_STATE = 16
        D_CONV = 4
        EXPAND = 2
        D_INNER = EXPAND * D_MODEL
        DT_RANK = D_MODEL // 16
        BATCH = 4
        SEQ = 512
        silu = jax.nn.silu
        xz = jnp.einsum('bld,ed->ble', x, W_in)
        xi, z = jnp.split(xz, 2, axis=-1)
        K = conv_w.shape[1]
        L = xi.shape[1]
        xpad = jnp.pad(xi, ((0, 0), (K - 1, 0), (0, 0)))
        xc = sum((xpad[:, k:k + L, :] * conv_w[:, k] for k in range(K)))
        u = silu(xc + conv_b)
        dbl = jnp.einsum('blc,ec->ble', u, W_xproj)
        dt = jax.nn.softplus(jnp.einsum('blr,cr->blc', dbl[..., :DT_RANK], W_dt) + b_dt)
        Bs = dbl[..., DT_RANK:DT_RANK + D_STATE]
        Cs = dbl[..., DT_RANK + D_STATE:]
        A = -jnp.exp(A_log)

        def step(h, inp):
            dt_t, B_t, C_t, u_t = inp
            dA = jnp.exp(dt_t[:, :, None] * A)
            h = h * dA + (dt_t * u_t)[:, :, None] * B_t[:, None, :]
            y = jnp.einsum('bcs,bs->bc', h, C_t)
            return (h, y)
        h0 = jnp.zeros((x.shape[0], D_INNER, D_STATE), x.dtype)
        xs = (jnp.swapaxes(dt, 0, 1), jnp.swapaxes(Bs, 0, 1), jnp.swapaxes(Cs, 0, 1), jnp.swapaxes(u, 0, 1))
        _, ys = jax.lax.scan(step, h0, xs)
        y = jnp.swapaxes(ys, 0, 1) + u * D_skip
        y = y * silu(z)
        return jnp.einsum('blc,dc->bld', y, W_out)

    def _L0_ffn_ref(x, w_gate, w_up, w_down):
        import jax, jax.numpy as jnp
        import numpy as np
        DIM = 256
        HIDDEN = 768
        SCALE = 1.0 / 127.0

        def _dequant(w_int, dtype):
            return w_int.astype(dtype) * jnp.asarray(SCALE, dtype)
        wg = _dequant(w_gate, x.dtype)
        wu = _dequant(w_up, x.dtype)
        wd = _dequant(w_down, x.dtype)
        gate = jnp.einsum('bsd,hd->bsh', x, wg)
        up = jnp.einsum('bsd,hd->bsh', x, wu)
        h = jax.nn.silu(gate) * up
        return jnp.einsum('bsh,dh->bsd', h, wd)
    x = L0_attn_x
    x = _layernorm(x + _L0_attn_ref(x, L0_attn_W_in, L0_attn_conv_w, L0_attn_conv_b, L0_attn_W_xproj, L0_attn_W_dt, L0_attn_b_dt, L0_attn_A_log, L0_attn_D_skip, L0_attn_W_out), axis=-1)
    x = _layernorm(x + _L0_ffn_ref(x, L0_ffn_w_gate, L0_ffn_w_up, L0_ffn_w_down), axis=-1)
    return x

_drawn_inputs = setup_inputs


def setup_inputs(seed=0):
    import zlib

    import numpy as np

    out = dict(_drawn_inputs(seed))
    spreads = {'L0_attn_D_skip': (1.0, 0.2)}
    factors = {'L0_attn_conv_b': 4.852}
    for name, (base, spread) in spreads.items():
        noise = np.random.default_rng([zlib.crc32(name.encode()), seed]).standard_normal(out[name].shape)
        drawn = base * np.exp(spread * noise) if base else spread * noise
        out[name] = jnp.asarray(drawn.astype(out[name].dtype))
    for name, factor in factors.items():
        out[name] = (out[name] * factor).astype(out[name].dtype)
    return out
```

```python
from contextlib import ExitStack

import concourse.bass as bass
from concourse import mybir

P = 128
T = 512
TB = T // P
TS = 32
DM = 256
DI = 512
CB = DI // P
N = 16
R = 16
KW = 4
HD = 768
HB = HD // P
DH = DM // P
EPS = 1e-5
QUADS = CB * N // 4
STEPS = CB * N
EXP_LN_SET = "natural_log_exp_and_others"

ALU = mybir.AluOpType
ACT = mybir.ActivationFunctionType
F32 = mybir.dt.float32
I32 = mybir.dt.int32

PE_SIDE = {
    (0, 0): ("xi", 0), (0, 1): ("gT", 0), (0, 2): ("xi", 1), (0, 3): ("gT", 1),
    (1, 0): ("xi", 2), (1, 1): ("gT", 2), (1, 2): ("xi", 3), (1, 3): ("gT", 3),
    (2, 0): ("z", 0), (2, 1): ("out", 0), (2, 2): ("z", 1), (2, 3): ("out", 1),
    (3, 0): ("z", 2), (3, 1): ("out", 2), (3, 2): ("z", 3), (3, 3): ("out", 3),
    (5, 1): ("x1T", 0), (5, 2): ("xproj", 0), (5, 3): ("x1T", 1),
    (6, 1): ("dt", 0), (6, 2): ("gate", 0), (6, 3): ("up", 0),
    (7, 1): ("dt", 1), (7, 2): ("gate", 1), (7, 3): ("up", 1),
    (8, 1): ("dt", 2), (8, 2): ("gate", 2), (8, 3): ("up", 2),
    (9, 1): ("dt", 3), (9, 2): ("gate", 3), (9, 3): ("up", 3),
    (10, 1): ("gate", 4), (10, 2): ("up", 4), (11, 1): ("gate", 5), (11, 2): ("up", 5),
    (12, 1): ("down", 0), (12, 3): ("down", 1), (13, 1): ("down", 2), (13, 3): ("down", 3),
}
ACT_SIDE = {
    (0, 1): ("xi", 0), (0, 2): ("gT", 0), (0, 3): ("xi", 1),
    (1, 0): ("gT", 1), (1, 1): ("xi", 2), (1, 2): ("gT", 2), (1, 3): ("xi", 3),
    (2, 0): ("gT", 3), (2, 1): ("z", 0), (2, 3): ("z", 1), (3, 1): ("z", 2), (3, 3): ("z", 3),
    (4, 0): ("silu", 0),
    (5, 2): ("x1T", 0), (5, 3): ("xproj", 0), (6, 0): ("x1T", 1),
    (6, 3): ("tanh", 0), (7, 3): ("tanh", 1), (8, 3): ("tanh", 2), (9, 3): ("tanh", 3),
    (10, 2): ("tanh", 4), (11, 2): ("tanh", 5),
    (12, 0): ("log", 0), (13, 2): ("log", 1),
}
DVE_SIDE = {
    (0, 0): [("dt_half", 1)], (0, 2): [("conv", 0, 0)], (0, 3): [("conv", 0, 1)],
    (1, 0): [("conv", 1, 0)], (1, 1): [("conv", 1, 1), ("gate_y", 3)],
    (1, 2): [("conv", 2, 0)], (1, 3): [("conv", 2, 1)],
    (2, 0): [("conv", 3, 0)], (2, 1): [("conv", 3, 1)], (2, 2): [("r1", 0)],
    (3, 0): [("r1", 1)], (3, 2): [("r1", 2)], (4, 0): [("r1", 3)], (4, 3): [("norm1", 0)],
    (5, 1): [("gate_y", 0)], (6, 2): [("xb", 0)], (7, 0): [("gs", 0)], (7, 1): [("hid", 0)],
    (7, 2): [("xb", 1)], (8, 0): [("gs", 1)], (8, 1): [("hid", 1)],
    (8, 2): [("xb", 2)], (9, 0): [("gs", 2)], (9, 1): [("gate_y", 1), ("hid", 2)],
    (9, 2): [("xb", 3)], (9, 3): [("min", 0)], (10, 0): [("gs", 3)], (10, 1): [("hid", 3)],
    (10, 3): [("gs", 4)], (11, 0): [("hid", 4)], (11, 3): [("gs", 5)], (12, 0): [("hid", 5)],
    (12, 2): [("dt_half", 0), ("min", 1)],
    (12, 3): [("r2", 0)], (13, 1): [("gate_y", 2), ("r2", 1)], (13, 3): [("r2", 2)],
    (14, 1): [("r2", 3)], (15, 0): [("norm2", 0)],
}

class Chunk:

    def __init__(self, row, half):
        self.row, self.half = row, half

    def __add__(self, d):
        return Chunk(self.row, self.half + d)

    @property
    def parity(self):
        return self.half % 2

    def count(self, per, i):
        return self.row * (2 * per) + (self.half * per + i)

    def tokens(self):
        return self.row * (2 * T) + self.half * T


def wait(eng, sem, value):
    if not isinstance(value, int) or value > 0:
        eng.wait_ge(sem, value)


def decay_bank(parity, i):
    return (i + parity) % 3


def decay_before(parity, i):
    if i >= 3:
        return i - 3
    bank = decay_bank(parity, i)
    return max(j for j in range(STEPS) if decay_bank(1 - parity, j) == bank) - STEPS


def mamba_ffn(nc, x, xT, W_inT, conv_w, conv_b, W_xT, W_dtT, b_dt, A_log, D_skip, W_outT,
              w_gT, w_uT, w_dT, out):
    ROWS = x.shape[0] // (2 * T)
    bc_dram = nc.dram_tensor("bc_scratch", [2 * N, T], F32, kind="Internal").ap()
    with ExitStack() as ctx:
        def sb(name, shape, dt=F32):
            return ctx.enter_context(nc.sbuf_tensor(name, shape, dt))

        def pb(name):
            return ctx.enter_context(nc.psum_tensor(name, [P, 512], F32))

        def sem(name):
            return ctx.enter_context(nc.semaphore(name))

        w_in = sb("w_in", [P, DH, 2 * DI])
        w_x = sb("w_x", [P, CB, R + 2 * N])
        w_dt = sb("w_dt", [R, DI])
        w_out = sb("w_out", [P, CB, DM])
        w_g = sb("w_g", [P, DH, HD])
        w_u = sb("w_u", [P, DH, HD])
        w_d = sb("w_d", [P, HB, DM])
        cw = sb("cw", [P, CB, KW])
        cbias = sb("cbias", [P, CB])
        bdt = sb("bdt", [P, CB])
        dsk = sb("dsk", [P, CB])
        a_neg = sb("a_neg", [P, CB, N])
        ident = sb("ident", [P, P])
        diag_d = sb("diag_d", [P, CB, P])
        of_token = sb("of_token", [P, TS])
        half_neg = sb("half_neg", [P, TB])
        eps = sb("eps", [P, TB])
        spare = sb("spare", [P, 1])
        xt = sb("xt", [P, 2, DH, T])
        res = sb("res", [P, TB, DM])
        xi = sb("xi", [P, 2, KW - 1 + T])
        hist = sb("hist", [P, CB, KW - 1])
        acc = sb("acc", [P, CB, T])
        u = sb("u", [P, 2, CB, T])
        dt = sb("dt", [P, CB, T])
        dtu = sb("dtu", [P, CB, T])
        sz = sb("sz", [P, TB, DI])
        b_all = sb("b_all", [P, N, T])
        c_col = sb("c_col", [P, 4, N])
        diag_c = sb("diag_c", [P, 4, N, TS])
        dbl = sb("dbl", [R + 2 * N, T])
        drive = sb("drive", [P, 4, 2, T])
        h = sb("h", [P, 2, T, 4])
        state = sb("state", [P, STEPS])
        hT = sb("hT", [P, 4, T])
        yg = sb("yg", [P, TB, DI])
        hid = sb("hid", [P, HB, T])
        stats = sb("stats", [P, 2, TB, 6])
        mv = sb("mv", [P, 2, TB, 2])
        var = sb("var", [P, 2, TB])
        rstd = sb("rstd", [P, 2, TB])
        decay = [pb(f"decay{i}") for i in range(3)]
        tp = [pb(f"tp{i}") for i in range(2)]
        yb = pb("yb")
        bx = pb("bx")
        by = pb("by")

        l_w = sem("l_w"); l_xt = [sem("l_xt0"), sem("l_xt1")]; l_res = sem("l_res")
        st_bc = sem("st_bc"); l_c = sem("l_c"); l_b = [sem(f"l_b{g}") for g in range(4)]
        st_out = sem("st_out")
        p_t = sem("p_t"); p_y = sem("p_y"); p_xi = sem("p_xi"); p_z = sem("p_z"); p_x = sem("p_x")
        p_dt = sem("p_dt"); p_gT = sem("p_gT"); p_out = sem("p_out"); p_x1T = sem("p_x1T")
        p_gate = sem("p_gate"); p_up = sem("p_up"); p_down = sem("p_down")
        a_da = sem("a_da"); a_ev = sem("a_ev"); a_xi = sem("a_xi"); a_u = sem("a_u"); a_z = sem("a_z")
        a_sz = sem("a_sz"); a_dbl = sem("a_dbl"); a_e = sem("a_e"); a_ln = sem("a_ln")
        a_gT = sem("a_gT"); a_x1T = sem("a_x1T"); a_th = sem("a_th"); a_set = sem("a_set")
        v_h = sem("v_h"); v_st = sem("v_st"); v_yg = sem("v_yg"); v_conv = sem("v_conv")
        v_xb = sem("v_xb"); v_mn = sem("v_mn"); v_dt = sem("v_dt"); v_dtu = sem("v_dtu")
        v_r1 = sem("v_r1"); v_s1 = sem("v_s1"); v_x1 = sem("v_x1"); v_gs = sem("v_gs")
        v_hid = sem("v_hid"); v_r2 = sem("v_r2"); v_s2 = sem("v_s2"); v_o = sem("v_o")
        v_set = sem("v_set")
        g_set = sem("g_set"); g_dr = sem("g_dr"); g_dc = sem("g_dc")
        g_n = [sem("g_n1"), sem("g_n2")]

        loads = [
            (w_in[:, :, :], W_inT.rearrange("(a p) n -> p a n", p=P)),
            (w_x[:, :, :], W_xT.rearrange("(a p) n -> p a n", p=P)),
            (w_dt[:, :], W_dtT),
            (w_out[:, :, :], W_outT.rearrange("(a p) n -> p a n", p=P)),
            (w_g[:, :, :].bitcast(I32), w_gT.rearrange("(a p) n -> p a n", p=P)),
            (w_u[:, :, :].bitcast(I32), w_uT.rearrange("(a p) n -> p a n", p=P)),
            (w_d[:, :, :].bitcast(I32), w_dT.rearrange("(a p) n -> p a n", p=P)),
            (cw[:, :, :], conv_w.rearrange("(a p) n -> p a n", p=P)),
            (cbias[:, :], conv_b),
            (bdt[:, :], b_dt),
            (dsk[:, :], D_skip),
            (a_neg[:, :, :], A_log.rearrange("(a p) n -> p a n", p=P)),
        ]
        ALL_LOADED = 16 * len(loads)
        SETUP_V = 8

        block = ctx.enter_context(nc.Block())

        @block.sync
        def _(eng):
            def load_xt(k):
                eng.dma_start(xt[:, k.parity, :, :],
                              xT[:, bass.ds(k.tokens(), T)].rearrange("(a p) t -> p a t", p=P))\
                   .then_inc(l_xt[k.parity], 16)

            def spread_bc(k):
                wait(eng, a_dbl, k.count(1, 1))
                eng.dma_start(bc_dram, dbl[R:R + 2 * N, :]).then_inc(st_bc, 16)
                wait(eng, st_bc, k.count(16, 16))
                for n in range(N):
                    g, s = n // 4, n % 4
                    eng.dma_start(c_col[s:P - 3 + s:4, g, :], bc_dram[N + n, :].rearrange("(b t) -> t b", t=TS),
                                  allow_slow_non_contiguous=True).then_inc(l_c, 16)

            def load_b(g):
                src = bc_dram[4 * g:4 * g + 4, :].rearrange("(o n) t -> o n t", o=1)
                eng.dma_start(b_all[:, 4 * g:4 * g + 4, :], src.to_broadcast([P, 4, T]))\
                   .then_inc(l_b[g], 16)

            def store(k):
                wait(eng, v_o, k.count(4, 4))
                eng.dma_start(out[bass.ds(k.tokens(), T), :].rearrange("(a p) d -> p a d", p=P),
                              res[:, :, :]).then_inc(st_out, 16)

            def load_res(k):
                wait(eng, st_out, k.count(16, 0))
                eng.dma_start(res[:, :, :],
                              x[bass.ds(k.tokens(), T), :].rearrange("(a p) d -> p a d", p=P))\
                   .then_inc(l_res, 16)

            def chunk(k, tail, head, more):
                if tail:
                    load_res(k + -1)
                if head:
                    spread_bc(k + 1)
                if more:
                    if tail:
                        wait(eng, p_up, k.count(6, 0))
                    else:
                        wait(eng, p_z, k.count(4, 4))
                    load_xt(k + 2)
                if head:
                    for g in range(4):
                        wait(eng, g_dr, k.count(32, 24 + 2 * g + 2))
                        load_b(g)
                if tail:
                    store(k + -1)

            for dst, src in loads:
                eng.dma_start(dst, src).then_inc(l_w, 16)
            load_xt(Chunk(0, 0))
            load_xt(Chunk(0, 1))
            spread_bc(Chunk(0, 0))
            for g in range(4):
                load_b(g)
            for half in range(2):
                chunk(Chunk(0, half), half == 1, True, True)
            with eng.Fori(1, ROWS - 1) as row:
                for half in range(2):
                    chunk(Chunk(row, half), True, True, True)
            for half in range(2):
                chunk(Chunk(ROWS - 1, half), True, half == 0, False)
            kl = Chunk(ROWS - 1, 1)
            load_res(kl)
            store(kl)
            eng.wait_ge(st_out, 2 * ROWS * 16)

        @block.gpsimd
        def _(eng):
            def drive_unit(k, j):
                cb, n = j // 8, 2 * (j % 8)
                wait(eng, v_h, k.count(STEPS, 2 * (j - 4) + 2))
                if cb == 0 and n % 4 == 0:
                    wait(eng, l_b[n // 4], k.count(16, 16))
                if j % 16 == 0:
                    wait(eng, v_dtu, k.count(2, j // 16 + 1))
                src = dtu[:, cb, :].rearrange("p (o t) -> p o t", o=1).to_broadcast([P, 2, T])
                nc.gpsimd.tensor_tensor(drive[:, j % 4, :, :], src, b_all[:, n:n + 2, :],
                                        ALU.mult).then_inc(g_dr, 1)

            def diagonals(k, g):
                if g == 0:
                    wait(eng, l_c, k.count(16 * N, 16 * N))
                wait(eng, p_y, k.count(64, -64 + 4 * (12 + g) + 4))
                mask = of_token[:, :].rearrange("p (o t) -> p o t", o=1).to_broadcast([P, N, TS])
                col = c_col[:, g, :].rearrange("p (b o) -> p b o", o=1).to_broadcast([P, N, TS])
                nc.gpsimd.tensor_tensor(diag_c[:, g, :, :], mask, col, ALU.mult).then_inc(g_dc, 1)

            def inverse_std(k, norm):
                wait(eng, (v_s1, v_s2)[norm], k.count(8, 8))
                nc.gpsimd.tensor_tensor(var[:, norm, :], mv[:, norm, :, 1], eps[:, :], ALU.add)\
                  .then_inc(g_n[norm], 1)
                eng.wait_ge(g_n[norm], k.count(2, 1))
                nc.gpsimd.tensor_tensor(rstd[:, norm, :], var[:, norm, :], half_neg[:, :], ALU.pow)\
                  .then_inc(g_n[norm], 1)

            def chunk(k, tail, head):
                for q in range(QUADS):
                    drive_unit(k, 2 * q)
                    drive_unit(k, 2 * q + 1)
                    if q in (0, 1):
                        diagonals(k, q + 2)
                    if q == 4 and tail:
                        inverse_std(k + -1, 0)
                    if q == 14 and tail:
                        inverse_std(k + -1, 1)
                    if q in (14, 15) and head:
                        diagonals(k + 1, q - 14)

            nc.gpsimd.memset(ident[:, :], 0.0).then_inc(g_set, 1)
            nc.gpsimd.memset(half_neg[:, :], -0.5).then_inc(g_set, 1)
            nc.gpsimd.memset(eps[:, :], EPS).then_inc(g_set, 1)
            nc.gpsimd.memset(of_token[:, :], 1.0).then_inc(g_set, 1)
            eng.wait_ge(g_set, 4)
            nc.gpsimd.affine_select(out=ident[:, :], in_=ident[:, :], compare_op=ALU.not_equal, fill=1.0,
                                    base=0, pattern=[[-1, P]], channel_multiplier=1).then_inc(g_set, 1)
            eng.wait_ge(g_set, 5)
            for base, sign in ((0, 1), (3, -1)):
                nc.gpsimd.affine_select(out=of_token[:, :], in_=of_token[:, :], compare_op=ALU.is_ge,
                                        fill=0.0, base=base, pattern=[[-4 * sign, TS]],
                                        channel_multiplier=sign).then_inc(g_set, 1)
                eng.wait_ge(g_set, 6 if sign > 0 else 7)
            diagonals(Chunk(0, 0), 0)
            diagonals(Chunk(0, 0), 1)
            for half in range(2):
                chunk(Chunk(0, half), half == 1, True)
            with eng.Fori(1, ROWS - 1) as row:
                for half in range(2):
                    chunk(Chunk(row, half), True, True)
            for half in range(2):
                chunk(Chunk(ROWS - 1, half), True, half == 0)
            inverse_std(Chunk(ROWS - 1, 1), 0)
            inverse_std(Chunk(ROWS - 1, 1), 1)

        @block.scalar
        def _(eng):
            act = nc.scalar.activation

            def decay_step(k, i):
                cb, n = i // N, i % N
                wait(eng, v_h, k.count(STEPS, decay_before(k.parity, i) + 1))
                if i % 32 == 0:
                    wait(eng, v_dt, k.count(2, i // 32 + 1))
                act(decay[decay_bank(k.parity, i)][:, :], dt[:, cb, :], ACT.Exp,
                    scale=a_neg[:, cb, n:n + 1]).then_inc(a_da, 1)

            def evacuate(k, g):
                wait(eng, p_t, k.count(64, g + 1))
                wait(eng, p_y, k.count(64, g - 3))
                act(hT[:, g % 4, :], tp[g % 2][:, :], ACT.Copy).then_inc(a_ev, 1)

            def copy_xi(k, cb):
                wait(eng, p_xi, k.count(4, cb + 1))
                if cb >= 2:
                    wait(eng, v_conv, k.count(24, 6 * (cb - 1)))
                else:
                    wait(eng, v_dt, k.count(2, 0))
                act(xi[:, cb % 2, KW - 1:], bx[:, :], ACT.Copy).then_inc(a_xi, 1)

            def copy_z(k, tb):
                wait(eng, p_z, k.count(4, tb + 1))
                wait(eng, v_yg, k.count(4, 0))
                act(sz[:, tb, :], bx[:, :], ACT.Copy).then_inc(a_z, 1)

            def silu_u(k):
                wait(eng, v_conv, k.count(24, 24))
                wait(eng, p_y, k.count(64, -64))
                act(u[:, k.parity, :, :], acc[:, :, :], ACT.Silu).then_inc(a_u, 1)

            def silu_z(k):
                eng.wait_ge(a_z, k.count(4, 4))
                act(sz[:, :, :], sz[:, :, :], ACT.Silu).then_inc(a_sz, 1)

            def copy_dbl(k):
                wait(eng, p_x, k.count(1, 1))
                wait(eng, st_bc, k.count(16, 0))
                act(dbl[:, :], bx[0:R + 2 * N, :], ACT.Copy).then_inc(a_dbl, 1)

            def softplus_log(k, half):
                tmp = xi[:, :, 0:T]
                wait(eng, v_mn, k.count(2, half + 1))
                act(tmp, tmp, ACT.Exp).then_inc(a_e, 1)
                eng.wait_ge(a_e, k.count(2, half + 1))
                act(tmp, tmp, ACT.Ln, bias=1.0).then_inc(a_ln, 1)

            def copy_gT(k, cb):
                wait(eng, p_gT, k.count(4, cb + 1))
                act(hid[:, cb, :], by[:, :], ACT.Copy).then_inc(a_gT, 1)

            def copy_x1T(k, dh):
                wait(eng, p_x1T, k.count(2, dh + 1))
                act(xt[:, (k.parity + 1) % 2, dh, :], by[:, :], ACT.Copy).then_inc(a_x1T, 1)

            def tanh_gate(k, m):
                wait(eng, p_gate, k.count(6, m + 1))
                act(hid[:, m, :], bx[:, :], ACT.Tanh, scale=0.5).then_inc(a_th, 1)

            def side(k, q, j, tail, head):
                what, i = ACT_SIDE.get((q, j), (None, 0))
                if what == "xi" and head:
                    copy_xi(k + 1, i)
                if what == "z":
                    copy_z(k, i)
                if what == "silu":
                    if head:
                        silu_u(k + 1)
                    silu_z(k)
                if what == "xproj" and head:
                    copy_dbl(k + 1)
                if what == "log" and head:
                    if i == 0:
                        nc.scalar.preload_act_table_set(EXP_LN_SET)
                    softplus_log(k + 1, i)
                if what == "gT" and tail:
                    copy_gT(k + -1, i)
                if what == "x1T" and tail:
                    copy_x1T(k + -1, i)
                if what == "tanh" and tail:
                    tanh_gate(k + -1, i)

            def chunk(k, tail, head, first=False):
                for q in range(QUADS):
                    for j in range(4):
                        i = 4 * q + 2 + j
                        if i < STEPS:
                            decay_step(k, i)
                        elif head:
                            decay_step(k + 1, i - STEPS)
                        if q >= 1:
                            evacuate(k, 4 * (q - 1) + j)
                        elif not first:
                            evacuate(k + -1, 60 + j)
                        side(k, q, j, tail, head)

            eng.wait_ge(l_w, ALL_LOADED)
            act(a_neg[:, :, :], a_neg[:, :, :], ACT.Exp).then_inc(a_set, 1)
            k0 = Chunk(0, 0)
            for cb in range(CB):
                copy_xi(k0, cb)
            silu_u(k0)
            copy_dbl(k0)
            nc.scalar.preload_act_table_set(EXP_LN_SET)
            for half in range(2):
                softplus_log(k0, half)
            eng.wait_ge(v_set, SETUP_V)
            decay_step(k0, 0)
            decay_step(k0, 1)
            for half in range(2):
                chunk(Chunk(0, half), half == 1, True, half == 0)
            with eng.Fori(1, ROWS - 1) as row:
                for half in range(2):
                    chunk(Chunk(row, half), True, True)
            for half in range(2):
                chunk(Chunk(ROWS - 1, half), True, half == 0)
            kl = Chunk(ROWS - 1, 1)
            for g in range(60, 64):
                evacuate(kl, g)
            for cb in range(CB):
                copy_gT(kl, cb)
            for dh in range(DH):
                copy_x1T(kl, dh)
            for m in range(HB):
                tanh_gate(kl, m)

        @block.vector
        def _(eng):
            tt, ts, stt = nc.vector.tensor_tensor, nc.vector.tensor_scalar, nc.vector.scalar_tensor_tensor

            def scan(k, i):
                q = i // 4
                wait(eng, a_da, k.count(STEPS, i + 1))
                if i % 2 == 0:
                    wait(eng, g_dr, k.count(32, i // 2 + 1))
                if i % 4 == 0:
                    wait(eng, p_t, k.count(64, 4 * (q - 1)))
                start = 0.0
                if k.parity:
                    start = state[:, i:i + 1]
                    if i == 0:
                        eng.wait_ge(v_st, k.count(QUADS // 2, QUADS // 2))
                elif i % 4 == 0 and q >= 2:
                    eng.wait_ge(v_st, k.count(QUADS // 2, q - 1))
                nc.vector.tensor_tensor_scan(h[:, q % 2, :, i % 4], decay[decay_bank(k.parity, i)][:, :],
                                             drive[:, (i // 2) % 4, i % 2, :], start, ALU.mult, ALU.add)\
                  .then_inc(v_h, 1)

            def save_state(k, q):
                eng.wait_ge(v_h, k.count(STEPS, 4 * q + 4))
                nc.vector.tensor_copy(state[:, 4 * q:4 * q + 4], h[:, q % 2, T - 1, :]).then_inc(v_st, 1)

            def gate_y(k, cb):
                wait(eng, p_y, k.count(64, 16 * (cb + 1)))
                if cb == 0:
                    wait(eng, a_sz, k.count(1, 1))
                    wait(eng, p_gT, k.count(4, 0))
                cols = slice(cb * P, (cb + 1) * P)
                tt(yg[:, :, cols], yb[:, :].rearrange("p (a c) -> p a c", c=P), sz[:, :, cols], ALU.mult)\
                    .then_inc(v_yg, 1)

            def conv(k, cb, part):
                s = cb % 2
                done = 6 * cb
                if part == 0:
                    wait(eng, v_conv, k.count(24, done))
                    wait(eng, v_dtu, k.count(2, 0))
                    if k.parity:
                        nc.vector.tensor_copy(xi[:, s, 0:KW - 1], hist[:, cb, :]).then_inc(v_conv, 1)
                    else:
                        nc.vector.memset(xi[:, s, 0:KW - 1], 0.0).then_inc(v_conv, 1)
                    wait(eng, a_xi, k.count(4, cb + 1))
                    wait(eng, a_u, k.count(1, 0))
                    eng.wait_ge(v_conv, k.count(24, done + 1))
                    nc.vector.tensor_copy(hist[:, cb, :], xi[:, s, T:T + KW - 1])\
                      .then_inc(v_conv, 1)
                    ts(acc[:, cb, :], xi[:, s, 3:3 + T], cw[:, cb, 3:4], cbias[:, cb:cb + 1],
                       ALU.mult, ALU.add).then_inc(v_conv, 1)
                    taps = (2,)
                else:
                    taps = (1, 0)
                for tap in taps:
                    eng.wait_ge(v_conv, k.count(24, done + 5 - tap))
                    stt(acc[:, cb, :], xi[:, s, tap:tap + T], cw[:, cb, tap:tap + 1], acc[:, cb, :],
                        ALU.mult, ALU.add).then_inc(v_conv, 1)

            def add_bias(k, cb):
                wait(eng, p_dt, k.count(4, cb + 1))
                if cb == 0:
                    wait(eng, a_u, k.count(1, 1))
                ts(acc[:, cb, :], bx[:, :], bdt[:, cb:cb + 1], None, ALU.add).then_inc(v_xb, 1)

            def clamp(k, half):
                eng.wait_ge(v_xb, k.count(4, 2 * half + 2))
                if half == 1:
                    eng.wait_ge(v_dt, k.count(2, 1))
                else:
                    eng.wait_ge(v_conv, k.count(24, 24))
                ts(xi[:, :, 0:T], acc[:, 2 * half:2 * half + 2, :], 40.0, None, ALU.min).then_inc(v_mn, 1)

            def dt_half(k, half):
                two = slice(2 * half, 2 * half + 2)
                wait(eng, a_ln, k.count(2, half + 1))
                wait(eng, a_da, k.count(STEPS, -STEPS + 32 * (half + 1)))
                tt(dt[:, two, :], acc[:, two, :], xi[:, :, 0:T], ALU.max).then_inc(v_dt, 1)
                eng.wait_ge(v_dt, k.count(2, half + 1))
                wait(eng, a_u, k.count(1, 1))
                wait(eng, g_dr, k.count(32, -32 + 16 * (half + 1)))
                tt(dtu[:, two, :], dt[:, two, :], u[:, k.parity, two, :], ALU.mult).then_inc(v_dtu, 1)

            def add_and_stats(k, tb, norm, ready, bank, done, stat):
                wait(eng, ready, k.count(4, tb + 1))
                if norm == 0 and tb == 0:
                    wait(eng, l_res, k.count(16, 16))
                tt(res[:, tb, :], bank[:, 0:DM], res[:, tb, :], ALU.add).then_inc(done, 1)
                eng.wait_ge(done, k.count(4, tb + 1))
                nc.vector.bn_stats(stats[:, norm, tb, :], res[:, tb, :]).then_inc(stat, 1)
                eng.wait_ge(stat, k.count(8, 2 * tb + 1))
                nc.vector.memset(spare[:, :], 0.0)
                nc.vector.bn_aggr(mv[:, norm, tb, :], stats[:, norm, tb, :]).then_inc(stat, 1)

            def normalise(k, norm, done):
                wait(eng, g_n[norm], k.count(2, 2))
                for tb in range(TB):
                    ts(res[:, tb, :], res[:, tb, :], mv[:, norm, tb, 0:1], rstd[:, norm, tb:tb + 1],
                       ALU.subtract, ALU.mult).then_inc(done, 1)

            def gate_silu(k, m):
                wait(eng, a_th, k.count(6, m + 1))
                stt(hid[:, m, :], hid[:, m, :], 1.0, bx[:, :], ALU.add, ALU.mult).then_inc(v_gs, 1)

            def hidden(k, m):
                wait(eng, p_up, k.count(6, m + 1))
                eng.wait_ge(v_gs, k.count(6, m + 1))
                tt(hid[:, m, :], by[:, :], hid[:, m, :], ALU.mult).then_inc(v_hid, 1)

            def side(k, q, j, tail, head, first):
                for what, i, *part in DVE_SIDE.get((q, j), []):
                    if what == "dt_half":
                        if i == 1:
                            dt_half(k, 1)
                        elif head:
                            dt_half(k + 1, 0)
                    if what == "conv" and head:
                        conv(k + 1, i, part[0])
                    if what == "gate_y":
                        if i < 3:
                            gate_y(k, i)
                        elif not first:
                            gate_y(k + -1, 3)
                    if what == "xb" and head:
                        add_bias(k + 1, i)
                    if what == "min" and head:
                        clamp(k + 1, i)
                    if what == "r1" and tail:
                        add_and_stats(k + -1, i, 0, p_out, by, v_r1, v_s1)
                    if what == "norm1" and tail:
                        normalise(k + -1, 0, v_x1)
                    if what == "gs" and tail:
                        gate_silu(k + -1, i)
                    if what == "hid" and tail:
                        hidden(k + -1, i)
                    if what == "r2" and tail:
                        add_and_stats(k + -1, i, 1, p_down, (by, bx)[i % 2], v_r2, v_s2)
                    if what == "norm2" and tail:
                        normalise(k + -1, 1, v_o)

            def chunk(k, tail, head, first=False):
                for q in range(QUADS):
                    for j in range(4):
                        scan(k, 4 * q + j)
                        side(k, q, j, tail, head, first)
                    if not k.parity:
                        save_state(k, q)

            eng.wait_ge(l_w, ALL_LOADED)
            for w, s in ((w_g, 1.0 / 127.0), (w_u, 1.0 / 127.0)):
                ts(w[:, :, :], w[:, :, :].bitcast(I32), s, None, ALU.mult).then_inc(v_set, 1)
            ts(w_d[:, :, :], w_d[:, :, :].bitcast(I32), 1.0 / 127.0, 0.5, ALU.mult, ALU.mult)\
                .then_inc(v_set, 1)
            eng.wait_ge(g_set, 5)
            for cb in range(CB):
                ts(diag_d[:, cb, :], ident[:, :], dsk[:, cb:cb + 1], None, ALU.mult).then_inc(v_set, 1)
            eng.wait_ge(a_set, 1)
            ts(a_neg[:, :, :], a_neg[:, :, :], -1.0, None, ALU.mult).then_inc(v_set, 1)
            k0 = Chunk(0, 0)
            for cb in range(CB):
                conv(k0, cb, 0)
                conv(k0, cb, 1)
            for cb in range(CB):
                add_bias(k0, cb)
            clamp(k0, 0)
            dt_half(k0, 0)
            clamp(k0, 1)
            for half in range(2):
                chunk(Chunk(0, half), half == 1, True, half == 0)
            with eng.Fori(1, ROWS - 1) as row:
                for half in range(2):
                    chunk(Chunk(row, half), True, True)
            for half in range(2):
                chunk(Chunk(ROWS - 1, half), True, half == 0)
            kl = Chunk(ROWS - 1, 1)
            gate_y(kl, 3)
            for tb in range(TB):
                add_and_stats(kl, tb, 0, p_out, by, v_r1, v_s1)
            normalise(kl, 0, v_x1)
            for m in range(HB):
                gate_silu(kl, m)
                hidden(kl, m)
            for tb in range(TB):
                add_and_stats(kl, tb, 1, p_down, (by, bx)[tb % 2], v_r2, v_s2)
            normalise(kl, 1, v_o)

        @block.tensor
        def _(eng):
            mm = nc.tensor.matmul

            def transposes(k, g):
                q, f = g // 4, g % 4
                if f == 0:
                    wait(eng, v_h, k.count(STEPS, 4 * q + 4))
                wait(eng, a_ev, k.count(64, g - 1))
                for b in range(4):
                    t0 = (4 * f + b) * TS
                    last = nc.tensor.transpose(tp[g % 2][:, b * P:(b + 1) * P],
                                               h[:, q % 2, t0:t0 + TS, :].rearrange("p t s -> p (t s)"), ident[:, :])
                last.then_inc(p_t, 1)

            def skip_term(k, cb):
                wait(eng, v_yg, k.count(4, cb))
                wait(eng, a_u, k.count(1, 1))
                for tb in range(TB):
                    mm(yb[:, tb * P:(tb + 1) * P], u[:, k.parity, cb, tb * P:(tb + 1) * P],
                       diag_d[:, cb, :], start=tb == 0, stop=False, skip_group_check=True)

            def sum_states(k, g):
                q, f = g // 4, g % 4
                if g % 16 == 0:
                    skip_term(k, g // 16)
                if g < 16 and f == 0:
                    wait(eng, g_dc, k.count(4, q + 1))
                wait(eng, a_ev, k.count(64, g + 1))
                for b in range(4):
                    last = mm(yb[b * TS:(b + 1) * TS, f * P:(f + 1) * P], diag_c[:, q % 4, 4 * f + b, :],
                              hT[:, g % 4, b * P:(b + 1) * P], start=False, stop=q % 4 == 3,
                              skip_group_check=True)
                last.then_inc(p_y, 1)

            def product(bank, pairs, done):
                for i, (lhsT, rhs) in enumerate(pairs):
                    last = mm(bank, lhsT, rhs, start=i == 0, stop=i == len(pairs) - 1)
                last.then_inc(done, 1)

            def in_xi(k, cb, tail_before):
                if cb == 0:
                    wait(eng, l_xt[k.parity], k.row * 16 + (k.half // 2 + 1) * 16)
                    if tail_before:
                        wait(eng, v_r2, k.count(4, -8))
                    else:
                        wait(eng, v_xb, k.count(4, 0))
                else:
                    wait(eng, a_xi, k.count(4, cb))
                product(bx[:, :], [(w_in[:, d, cb * P:(cb + 1) * P], xt[:, k.parity, d, :])
                                   for d in range(DH)], p_xi)

            def in_z(k, tb, head):
                if tb == 0 and head:
                    wait(eng, a_xi, k.count(4, 8))
                if tb == 0 and not head:
                    wait(eng, v_r2, k.count(4, -4))
                if tb > 0:
                    wait(eng, a_z, k.count(4, tb))
                product(bx[:, :], [(xt[:, k.parity, d, tb * P:(tb + 1) * P], w_in[:, d, DI:2 * DI])
                                   for d in range(DH)], p_z)

            def x_proj(k, z_before):
                wait(eng, a_z, z_before)
                wait(eng, a_xi, k.count(4, 4))
                wait(eng, a_u, k.count(1, 1))
                product(bx[0:R + 2 * N, :], [(w_x[:, c, :], u[:, k.parity, c, :]) for c in range(CB)], p_x)

            def dt_proj(k, cb, tail):
                if cb == 0:
                    wait(eng, a_dbl, k.count(1, 1))
                else:
                    wait(eng, v_xb, k.count(4, cb))
                    if tail:
                        wait(eng, v_gs, (k + -2).count(6, cb))
                product(bx[:, :], [(w_dt[:, cb * P:(cb + 1) * P], dbl[0:R, :])], p_dt)

            def turn_gated(k, cb):
                wait(eng, v_yg, k.count(4, cb + 1))
                if cb == 0:
                    wait(eng, v_r2, k.count(4, -1))
                else:
                    wait(eng, a_gT, k.count(4, cb))
                for tb in range(TB):
                    last = nc.tensor.transpose(by[:, tb * P:(tb + 1) * P],
                                               yg[:, tb, cb * P:(cb + 1) * P], ident[:, :])
                last.then_inc(p_gT, 1)

            def out_proj(k, tb):
                if tb == 0:
                    wait(eng, a_gT, k.count(4, 4))
                else:
                    wait(eng, v_r1, k.count(4, tb))
                product(by[:, 0:DM], [(hid[:, c, tb * P:(tb + 1) * P], w_out[:, c, :])
                                      for c in range(CB)], p_out)

            def turn_x1(k, dh):
                if dh == 0:
                    wait(eng, v_x1, k.count(4, 4))
                else:
                    wait(eng, a_x1T, k.count(2, 1))
                for tb in range(TB):
                    last = nc.tensor.transpose(by[:, tb * P:(tb + 1) * P],
                                               res[:, tb, dh * P:(dh + 1) * P], ident[:, :])
                last.then_inc(p_x1T, 1)

            def gate_up(k, m, weight, bank, done):
                x1 = xt[:, (k.parity + 1) % 2, :, :]
                product(bank[:, :], [(weight[:, d, m * P:(m + 1) * P], x1[:, d, :])
                                     for d in range(DH)], done)

            def gate(k, m, dt_between, before):
                if m == 0:
                    wait(eng, a_x1T, k.count(2, 2))
                if dt_between and m < CB:
                    wait(eng, v_xb, (k + 2).count(4, m + 1))
                elif m > 0:
                    wait(eng, v_gs, k.count(6, m))
                else:
                    wait(eng, *before)
                gate_up(k, m, w_g, bx, p_gate)

            def up(k, m):
                if m == 0:
                    wait(eng, a_x1T, k.count(2, 2))
                else:
                    wait(eng, v_hid, k.count(6, m))
                gate_up(k, m, w_u, by, p_up)

            def down(k, tb):
                if tb < 2:
                    wait(eng, v_hid, k.count(6, 6))
                else:
                    wait(eng, v_r2, k.count(4, tb - 1))
                product((by, bx)[tb % 2][:, 0:DM], [(hid[:, m, tb * P:(tb + 1) * P], w_d[:, m, :])
                                                    for m in range(HB)], p_down)

            def side(k, q, j, tail, head, tail_before):
                what, i = PE_SIDE.get((q, j), (None, 0))
                if what == "xi" and head:
                    in_xi(k + 1, i, tail_before)
                if what == "z":
                    in_z(k, i, head)
                if what == "xproj" and head:
                    x_proj(k + 1, k.count(4, 4))
                if what == "dt" and head:
                    dt_proj(k + 1, i, tail)
                if what == "gT" and tail:
                    turn_gated(k + -1, i)
                if what == "out" and tail:
                    out_proj(k + -1, i)
                if what == "x1T" and tail:
                    turn_x1(k + -1, i)
                if what == "gate" and tail:
                    gate(k + -1, i, head, (a_z, k.count(4, 4)))
                if what == "up" and tail:
                    up(k + -1, i)
                if what == "down" and tail:
                    down(k + -1, i)

            def chunk(k, tail, head, first=False, second=False):
                for q in range(QUADS):
                    for j in range(4):
                        g = 4 * (q - 1) + j
                        if g >= 0:
                            transposes(k, g)
                        elif not first:
                            transposes(k + -1, 64 + g)
                        side(k, q, j, tail, head, not (first or second))
                        if g >= 1:
                            sum_states(k, g - 1)
                        elif not first:
                            sum_states(k + -1, 63 + g)

            eng.wait_ge(l_w, ALL_LOADED)
            eng.wait_ge(g_set, 5)
            eng.wait_ge(v_set, SETUP_V)
            k0 = Chunk(0, 0)
            for cb in range(CB):
                in_xi(k0, cb, False)
            x_proj(k0, 0)
            for cb in range(CB):
                dt_proj(k0, cb, False)
            for half in range(2):
                chunk(Chunk(0, half), half == 1, True, half == 0, half == 1)
            with eng.Fori(1, ROWS - 1) as row:
                for half in range(2):
                    chunk(Chunk(row, half), True, True)
            for half in range(2):
                chunk(Chunk(ROWS - 1, half), True, half == 0)
            kl = Chunk(ROWS - 1, 1)
            for g in range(60, 64):
                transposes(kl, g)
                sum_states(kl, g - 1)
            sum_states(kl, 63)
            for cb in range(CB):
                turn_gated(kl, cb)
            for tb in range(TB):
                out_proj(kl, tb)
            for dh in range(DH):
                turn_x1(kl, dh)
            for m in range(HB):
                gate(kl, m, False, (v_r2, kl.count(4, 0)))
                up(kl, m)
            for tb in range(TB):
                down(kl, tb)


def kernel(L0_attn_x, L0_attn_W_in, L0_attn_conv_w, L0_attn_conv_b, L0_attn_W_xproj, L0_attn_W_dt,
           L0_attn_b_dt, L0_attn_A_log, L0_attn_D_skip, L0_attn_W_out, L0_ffn_w_gate, L0_ffn_w_up,
           L0_ffn_w_down):
    import numpy as np
    import concourse.bacc as bacc
    from concourse.bass_utils import run_bass_kernel_spmd

    def columns(v):
        return np.asarray(v).reshape(-1, P).T

    x = np.ascontiguousarray(L0_attn_x).reshape(-1, DM)
    arrays = {
        "x": x, "xT": x.T, "W_inT": L0_attn_W_in.T, "conv_w": L0_attn_conv_w, "conv_b": columns(L0_attn_conv_b),
        "W_xT": L0_attn_W_xproj.T, "W_dtT": L0_attn_W_dt.T, "b_dt": columns(L0_attn_b_dt), "A_log": L0_attn_A_log,
        "D_skip": columns(L0_attn_D_skip), "W_outT": L0_attn_W_out.T, "w_gT": L0_ffn_w_gate.T,
        "w_uT": L0_ffn_w_up.T, "w_dT": L0_ffn_w_down.T,
    }
    arrays = {f"in_{k}": np.ascontiguousarray(v) for k, v in arrays.items()}
    nc = bacc.Bacc("TRN2", target_bir_lowering=False, num_devices=1)
    args = [nc.dram_tensor(k, v.shape, mybir.dt.from_np(v.dtype), kind="ExternalInput").ap()
            for k, v in arrays.items()]
    out = nc.dram_tensor("out", x.shape, F32, kind="ExternalOutput").ap()
    mamba_ffn(nc, *args, out)
    got = run_bass_kernel_spmd(nc, [arrays], core_ids=[0]).results[0]["out"]
    return got.reshape(L0_attn_x.shape)
```

```python
from contextlib import ExitStack

import concourse.bass as bass
from concourse import mybir

P = 128
T = 512
TB = T // P
TS = 32
DM = 256
DI = 512
CB = DI // P
N = 16
R = 16
KW = 4
HD = 768
HB = HD // P
DH = DM // P
EPS = 1e-5
QUADS = CB * N // 4
STEPS = CB * N
EXP_LN_SET = "natural_log_exp_and_others"

ALU = mybir.AluOpType
ACT = mybir.ActivationFunctionType
F32 = mybir.dt.float32
I32 = mybir.dt.int32

PE_SIDE = {
    (0, 0): [("xi", 0)], (0, 1): [("gT", 0)], (0, 2): [("xi", 1)], (0, 3): [("gT", 1)],
    (1, 0): [("xi", 2)], (1, 1): [("gT", 2)], (1, 2): [("xi", 3)], (1, 3): [("gT", 3)],
    (2, 0): [("z", 0)], (2, 1): [("out", 0)], (2, 3): [("z", 1)],
    (3, 0): [("out", 1)], (3, 1): [("z", 2)], (3, 3): [("z", 3)],
    (4, 0): [("out", 2)], (4, 2): [("out", 3)], (5, 1): [("xproj", 0)],
    (5, 3): [("x1T", 0)], (6, 0): [("dt", 0)], (6, 1): [("dt", 1), ("x1T", 1)],
    (6, 2): [("dt", 2)], (6, 3): [("dt", 3)],
    (7, 1): [("gate", 0)], (7, 3): [("up", 0)], (8, 1): [("gate", 1)], (8, 3): [("up", 1)],
    (9, 1): [("gate", 2)], (9, 3): [("up", 2)], (10, 1): [("gate", 3)], (10, 3): [("up", 3)],
    (11, 1): [("gate", 4)], (11, 3): [("up", 4)], (12, 1): [("gate", 5)], (12, 3): [("up", 5)],
    (13, 2): [("down", 0)], (14, 0): [("down", 1)], (14, 2): [("down", 2)], (15, 1): [("down", 3)],
}
ACT_SIDE = {
    (0, 1): [("xi", 0)], (0, 2): [("gT", 0)], (0, 3): [("xi", 1)],
    (1, 0): [("gT", 1)], (1, 1): [("xi", 2)], (1, 2): [("gT", 2)], (1, 3): [("xi", 3)],
    (2, 0): [("gT", 3)], (2, 1): [("z", 0)], (3, 0): [("z", 1)], (3, 2): [("z", 2)],
    (4, 0): [("z", 3)],
    (5, 2): [("xproj", 0)], (6, 0): [("x1T", 0)], (6, 2): [("x1T", 1)],
    (7, 2): [("tanh", 0)], (8, 2): [("tanh", 1)], (9, 2): [("tanh", 2)], (10, 2): [("tanh", 3)],
    (11, 2): [("tanh", 4)], (12, 2): [("tanh", 5)],
    (13, 0): [("log", 0)], (14, 2): [("log", 1)],
}
SILU_QUAD = 4
SILU_ORDER = [
    ("side", 0), ("decay", 0), ("hT", 0), ("decay", 1), ("hT", 1), ("side", 1), ("decay", 2), ("side", 2),
    ("decay", 3), ("side", 3),
    ("u", 0), ("u", 1), ("hT", 2), ("u", 2), ("u", 3), ("hT", 3), ("sz", 0), ("sz", 1), ("hT", 4),
    ("sz", 2), ("sz", 3), ("decay", 4), ("side", 4), ("decay", 5), ("hT", 5), ("side", 5),
    ("decay", 6), ("hT", 6), ("side", 6), ("decay", 7), ("hT", 7), ("side", 7),
]
DVE_SIDE = {
    (0, 0): [("dt_half", 1)], (0, 2): [("conv", 0, 0)], (0, 3): [("conv", 0, 1)],
    (1, 0): [("conv", 1, 0), ("gate_y", 3)],
    (1, 1): [("conv", 1, 1)],
    (1, 2): [("norm2", 0), ("conv", 2, 0)], (1, 3): [("conv", 2, 1)],
    (2, 0): [("conv", 3, 0)], (2, 1): [("conv", 3, 1)], (2, 3): [("r1", 0)],
    (3, 1): [("r1", 1)], (4, 1): [("r1", 2)], (4, 3): [("r1", 3)], (5, 0): [("norm1", 0)],
    (5, 1): [("gate_y", 0)], (6, 1): [("xb", 0)], (6, 2): [("xb", 1)],
    (6, 3): [("xb", 2)], (7, 0): [("xb", 3)], (7, 1): [("min", 0)],
    (7, 3): [("gs", 0)], (8, 1): [("hid", 0)], (8, 3): [("gs", 1)], (9, 1): [("gate_y", 1), ("hid", 1)],
    (9, 3): [("gs", 2)], (10, 1): [("hid", 2)], (10, 3): [("gs", 3)], (11, 1): [("hid", 3)],
    (11, 3): [("gs", 4)], (12, 1): [("hid", 4)], (12, 3): [("gs", 5)], (13, 1): [("hid", 5), ("gate_y", 2)],
    (13, 3): [("dt_half", 0), ("min", 1)],
    (14, 0): [("r2", 0)], (14, 2): [("r2", 1)], (15, 0): [("r2", 2)], (15, 2): [("r2", 3)],
}

class Chunk:

    def __init__(self, row, half):
        self.row, self.half = row, half

    def __add__(self, d):
        return Chunk(self.row, self.half + d)

    @property
    def parity(self):
        return self.half % 2

    def count(self, per, i):
        return self.row * (2 * per) + (self.half * per + i)

    def tokens(self):
        return self.row * (2 * T) + self.half * T


def wait(eng, sem, value):
    if not isinstance(value, int) or value > 0:
        eng.wait_ge(sem, value)


def decay_bank(parity, i):
    return (i + parity) % 3


def decay_before(parity, i):
    if i >= 3:
        return i - 3
    bank = decay_bank(parity, i)
    return max(j for j in range(STEPS) if decay_bank(1 - parity, j) == bank) - STEPS


def mamba_ffn(nc, x, xT, W_inT, conv_w, conv_b, W_xT, W_dtT, b_dt, A_log, D_skip, W_outT,
              w_gT, w_uT, w_dT, out):
    ROWS = x.shape[0] // (2 * T)
    bc_dram = nc.dram_tensor("bc_scratch", [2 * N, T], F32, kind="Internal").ap()
    with ExitStack() as ctx:
        def sb(name, shape, dt=F32):
            return ctx.enter_context(nc.sbuf_tensor(name, shape, dt))

        def pb(name):
            return ctx.enter_context(nc.psum_tensor(name, [P, 512], F32))

        def sem(name):
            return ctx.enter_context(nc.semaphore(name))

        w_in = sb("w_in", [P, DH, 2 * DI])
        w_x = sb("w_x", [P, CB, R + 2 * N])
        w_dt = sb("w_dt", [R, DI])
        w_out = sb("w_out", [P, CB, DM])
        w_g = sb("w_g", [P, DH, HD])
        w_u = sb("w_u", [P, DH, HD])
        w_d = sb("w_d", [P, HB, DM])
        cw = sb("cw", [P, CB, KW])
        cbias = sb("cbias", [P, CB])
        bdt = sb("bdt", [P, CB])
        dsk = sb("dsk", [P, CB])
        a_neg = sb("a_neg", [P, CB, N])
        ident = sb("ident", [P, P])
        diag_d = sb("diag_d", [P, CB, P])
        of_token = sb("of_token", [P, TS])
        half_neg = sb("half_neg", [P, TB])
        eps = sb("eps", [P, TB])
        spare = sb("spare", [P, 1])
        xt = sb("xt", [P, 2, DH, T])
        res = sb("res", [P, TB, DM])
        xi = sb("xi", [P, 2, KW - 1 + T])
        hist = sb("hist", [P, CB, KW - 1])
        acc = sb("acc", [P, CB, T])
        u = sb("u", [P, 2, CB, T])
        dt = sb("dt", [P, CB, T])
        dtu = sb("dtu", [P, CB, T])
        sz = sb("sz", [P, TB, DI])
        b_all = sb("b_all", [P, N, T])
        c_col = sb("c_col", [P, 4, N])
        diag_c = sb("diag_c", [P, 4, N, TS])
        dbl = sb("dbl", [R + 2 * N, T])
        drive = sb("drive", [P, 4, 2, T])
        h = sb("h", [P, 2, T, 4])
        state = sb("state", [P, STEPS])
        hT = sb("hT", [P, 4, T])
        yg = sb("yg", [P, TB, DI])
        hid = sb("hid", [P, HB, T])
        stats = sb("stats", [P, 2, TB, 6])
        mv = sb("mv", [P, 2, TB, 2])
        var = sb("var", [P, 2, TB])
        rstd = sb("rstd", [P, 2, TB])
        decay = [pb(f"decay{i}") for i in range(3)]
        tp = [pb(f"tp{i}") for i in range(2)]
        yb = pb("yb")
        bx = pb("bx")
        by = pb("by")

        l_w = sem("l_w"); l_xt = [sem("l_xt0"), sem("l_xt1")]; l_res = sem("l_res")
        st_bc = sem("st_bc"); l_c = sem("l_c"); l_b = [sem(f"l_b{g}") for g in range(4)]
        st_out = sem("st_out")
        p_t = sem("p_t"); p_y = sem("p_y"); p_xi = sem("p_xi"); p_z = sem("p_z"); p_x = sem("p_x")
        p_dt = sem("p_dt"); p_gT = sem("p_gT"); p_out = sem("p_out"); p_x1T = sem("p_x1T")
        p_gate = sem("p_gate"); p_up = sem("p_up"); p_down = sem("p_down")
        a_da = sem("a_da"); a_ev = sem("a_ev"); a_xi = sem("a_xi"); a_u = sem("a_u"); a_z = sem("a_z")
        a_sz = sem("a_sz"); a_dbl = sem("a_dbl"); a_e = sem("a_e"); a_ln = sem("a_ln")
        a_gT = sem("a_gT"); a_x1T = sem("a_x1T"); a_th = sem("a_th"); a_set = sem("a_set")
        v_h = sem("v_h"); v_st = sem("v_st"); v_yg = sem("v_yg"); v_conv = sem("v_conv")
        v_xb = sem("v_xb"); v_mn = sem("v_mn"); v_dt = sem("v_dt"); v_dtu = sem("v_dtu")
        v_r1 = sem("v_r1"); v_s1 = sem("v_s1"); v_x1 = sem("v_x1"); v_gs = sem("v_gs")
        v_hid = sem("v_hid"); v_r2 = sem("v_r2"); v_s2 = sem("v_s2"); v_o = sem("v_o")
        v_set = sem("v_set")
        g_set = sem("g_set"); g_dr = sem("g_dr"); g_dc = sem("g_dc")
        g_n = [sem("g_n1"), sem("g_n2")]

        loads = [
            (w_in[:, :, :], W_inT.rearrange("(a p) n -> p a n", p=P)),
            (w_x[:, :, :], W_xT.rearrange("(a p) n -> p a n", p=P)),
            (w_dt[:, :], W_dtT),
            (w_out[:, :, :], W_outT.rearrange("(a p) n -> p a n", p=P)),
            (w_g[:, :, :].bitcast(I32), w_gT.rearrange("(a p) n -> p a n", p=P)),
            (w_u[:, :, :].bitcast(I32), w_uT.rearrange("(a p) n -> p a n", p=P)),
            (w_d[:, :, :].bitcast(I32), w_dT.rearrange("(a p) n -> p a n", p=P)),
            (cw[:, :, :], conv_w.rearrange("(a p) n -> p a n", p=P)),
            (cbias[:, :], conv_b),
            (bdt[:, :], b_dt),
            (dsk[:, :], D_skip),
            (a_neg[:, :, :], A_log.rearrange("(a p) n -> p a n", p=P)),
        ]
        ALL_LOADED = 16 * len(loads)
        SETUP_V = 8

        block = ctx.enter_context(nc.Block())

        @block.sync
        def _(eng):
            def load_xt(k):
                eng.dma_start(xt[:, k.parity, :, :],
                              xT[:, bass.ds(k.tokens(), T)].rearrange("(a p) t -> p a t", p=P))\
                   .then_inc(l_xt[k.parity], 16)

            def spread_bc(k):
                wait(eng, a_dbl, k.count(1, 1))
                eng.dma_start(bc_dram, dbl[R:R + 2 * N, :]).then_inc(st_bc, 16)
                wait(eng, st_bc, k.count(16, 16))
                for n in range(N):
                    g, s = n // 4, n % 4
                    eng.dma_start(c_col[s:P - 3 + s:4, g, :], bc_dram[N + n, :].rearrange("(b t) -> t b", t=TS),
                                  allow_slow_non_contiguous=True).then_inc(l_c, 16)

            def load_b(g):
                src = bc_dram[4 * g:4 * g + 4, :].rearrange("(o n) t -> o n t", o=1)
                eng.dma_start(b_all[:, 4 * g:4 * g + 4, :], src.to_broadcast([P, 4, T]))\
                   .then_inc(l_b[g], 16)

            def store(k):
                wait(eng, v_o, k.count(4, 4))
                eng.dma_start(out[bass.ds(k.tokens(), T), :].rearrange("(a p) d -> p a d", p=P),
                              res[:, :, :]).then_inc(st_out, 16)

            def load_res(k):
                wait(eng, st_out, k.count(16, 0))
                eng.dma_start(res[:, :, :],
                              x[bass.ds(k.tokens(), T), :].rearrange("(a p) d -> p a d", p=P))\
                   .then_inc(l_res, 16)

            def chunk(k, tail, head, more, late=True):
                if late:
                    store(k + -2)
                if tail:
                    load_res(k + -1)
                if head:
                    spread_bc(k + 1)
                if more:
                    if tail:
                        wait(eng, p_up, k.count(6, 0))
                    else:
                        wait(eng, p_z, k.count(4, 4))
                    load_xt(k + 2)
                if head:
                    for g in range(4):
                        wait(eng, g_dr, k.count(32, 24 + 2 * g + 2))
                        load_b(g)

            for dst, src in loads:
                eng.dma_start(dst, src).then_inc(l_w, 16)
            load_xt(Chunk(0, 0))
            load_xt(Chunk(0, 1))
            spread_bc(Chunk(0, 0))
            for g in range(4):
                load_b(g)
            for half in range(2):
                chunk(Chunk(0, half), half == 1, True, True, False)
            with eng.Fori(1, ROWS - 1) as row:
                for half in range(2):
                    chunk(Chunk(row, half), True, True, True)
            for half in range(2):
                chunk(Chunk(ROWS - 1, half), True, half == 0, False)
            kl = Chunk(ROWS - 1, 1)
            store(kl + -1)
            load_res(kl)
            store(kl)
            eng.wait_ge(st_out, 2 * ROWS * 16)

        @block.gpsimd
        def _(eng):
            def drive_unit(k, j):
                cb, n = j // 8, 2 * (j % 8)
                wait(eng, v_h, k.count(STEPS, 2 * (j - 4) + 2))
                if cb == 0 and n % 4 == 0:
                    wait(eng, l_b[n // 4], k.count(16, 16))
                if j % 16 == 0:
                    wait(eng, v_dtu, k.count(2, j // 16 + 1))
                src = dtu[:, cb, :].rearrange("p (o t) -> p o t", o=1).to_broadcast([P, 2, T])
                nc.gpsimd.tensor_tensor(drive[:, j % 4, :, :], src, b_all[:, n:n + 2, :],
                                        ALU.mult).then_inc(g_dr, 1)

            def diagonals(k, g):
                if g == 0:
                    wait(eng, l_c, k.count(16 * N, 16 * N))
                wait(eng, p_y, k.count(64, -64 + 4 * (12 + g) + 4))
                mask = of_token[:, :].rearrange("p (o t) -> p o t", o=1).to_broadcast([P, N, TS])
                col = c_col[:, g, :].rearrange("p (b o) -> p b o", o=1).to_broadcast([P, N, TS])
                nc.gpsimd.tensor_tensor(diag_c[:, g, :, :], mask, col, ALU.mult).then_inc(g_dc, 1)

            def inverse_std(k, norm):
                wait(eng, (v_s1, v_s2)[norm], k.count(8, 8))
                nc.gpsimd.tensor_tensor(var[:, norm, :], mv[:, norm, :, 1], eps[:, :], ALU.add)\
                  .then_inc(g_n[norm], 1)
                eng.wait_ge(g_n[norm], k.count(2, 1))
                nc.gpsimd.tensor_tensor(rstd[:, norm, :], var[:, norm, :], half_neg[:, :], ALU.pow)\
                  .then_inc(g_n[norm], 1)

            def chunk(k, tail, head, late=True):
                for q in range(QUADS):
                    drive_unit(k, 2 * q)
                    drive_unit(k, 2 * q + 1)
                    if q == 1 and late:
                        inverse_std(k + -2, 1)
                    if q == 4 and tail:
                        inverse_std(k + -1, 0)
                    if q in (0, 1):
                        diagonals(k, q + 2)
                    if q in (14, 15) and head:
                        diagonals(k + 1, q - 14)

            nc.gpsimd.memset(ident[:, :], 0.0).then_inc(g_set, 1)
            nc.gpsimd.memset(half_neg[:, :], -0.5).then_inc(g_set, 1)
            nc.gpsimd.memset(eps[:, :], EPS).then_inc(g_set, 1)
            nc.gpsimd.memset(of_token[:, :], 1.0).then_inc(g_set, 1)
            eng.wait_ge(g_set, 4)
            nc.gpsimd.affine_select(out=ident[:, :], in_=ident[:, :], compare_op=ALU.not_equal, fill=1.0,
                                    base=0, pattern=[[-1, P]], channel_multiplier=1).then_inc(g_set, 1)
            eng.wait_ge(g_set, 5)
            for base, sign in ((0, 1), (3, -1)):
                nc.gpsimd.affine_select(out=of_token[:, :], in_=of_token[:, :], compare_op=ALU.is_ge,
                                        fill=0.0, base=base, pattern=[[-4 * sign, TS]],
                                        channel_multiplier=sign).then_inc(g_set, 1)
                eng.wait_ge(g_set, 6 if sign > 0 else 7)
            diagonals(Chunk(0, 0), 0)
            diagonals(Chunk(0, 0), 1)
            for half in range(2):
                chunk(Chunk(0, half), half == 1, True, False)
            with eng.Fori(1, ROWS - 1) as row:
                for half in range(2):
                    chunk(Chunk(row, half), True, True)
            for half in range(2):
                chunk(Chunk(ROWS - 1, half), True, half == 0)
            inverse_std(Chunk(ROWS - 1, 0), 1)
            inverse_std(Chunk(ROWS - 1, 1), 0)
            inverse_std(Chunk(ROWS - 1, 1), 1)

        @block.scalar
        def _(eng):
            act = nc.scalar.activation

            def decay_step(k, i):
                cb, n = i // N, i % N
                wait(eng, v_h, k.count(STEPS, decay_before(k.parity, i) + 1))
                if i % 32 == 0:
                    wait(eng, v_dt, k.count(2, i // 32 + 1))
                act(decay[decay_bank(k.parity, i)][:, :], dt[:, cb, :], ACT.Exp,
                    scale=a_neg[:, cb, n:n + 1]).then_inc(a_da, 1)

            def evacuate(k, g):
                wait(eng, p_t, k.count(64, g + 1))
                wait(eng, p_y, k.count(64, g - 3))
                act(hT[:, g % 4, :], tp[g % 2][:, :], ACT.Copy).then_inc(a_ev, 1)

            def copy_xi(k, cb):
                wait(eng, p_xi, k.count(4, cb + 1))
                if cb >= 2:
                    wait(eng, v_conv, k.count(24, 6 * (cb - 1)))
                else:
                    wait(eng, v_dt, k.count(2, 0))
                act(xi[:, cb % 2, KW - 1:], bx[:, :], ACT.Copy).then_inc(a_xi, 1)

            def copy_z(k, tb):
                wait(eng, p_z, k.count(4, tb + 1))
                wait(eng, v_yg, k.count(4, 0))
                act(sz[:, tb, :], bx[:, :], ACT.Copy).then_inc(a_z, 1)

            def silu_u(k, cb):
                wait(eng, v_conv, k.count(24, 6 * (cb + 1)))
                wait(eng, p_y, k.count(64, -64))
                act(u[:, k.parity, cb, :], acc[:, cb, :], ACT.Silu).then_inc(a_u, 1)

            def silu_z(k, tb):
                eng.wait_ge(a_z, k.count(4, tb + 1))
                act(sz[:, tb, :], sz[:, tb, :], ACT.Silu).then_inc(a_sz, 1)

            def copy_dbl(k):
                wait(eng, p_x, k.count(1, 1))
                wait(eng, st_bc, k.count(16, 0))
                act(dbl[:, :], bx[0:R + 2 * N, :], ACT.Copy).then_inc(a_dbl, 1)

            def softplus_log(k, half):
                tmp = xi[:, :, 0:T]
                wait(eng, v_mn, k.count(2, half + 1))
                act(tmp, tmp, ACT.Exp).then_inc(a_e, 1)
                eng.wait_ge(a_e, k.count(2, half + 1))
                act(tmp, tmp, ACT.Ln, bias=1.0).then_inc(a_ln, 1)

            def copy_gT(k, cb):
                wait(eng, p_gT, k.count(4, cb + 1))
                act(hid[:, cb, :], by[:, :], ACT.Copy).then_inc(a_gT, 1)

            def copy_x1T(k, dh):
                wait(eng, p_x1T, k.count(2, dh + 1))
                act(xt[:, (k.parity + 1) % 2, dh, :], by[:, :], ACT.Copy).then_inc(a_x1T, 1)

            def tanh_gate(k, m):
                wait(eng, p_gate, k.count(6, m + 1))
                act(hid[:, m, :], bx[:, :], ACT.Tanh, scale=0.5).then_inc(a_th, 1)

            def side(k, q, j, tail, head):
                for what, i in ACT_SIDE.get((q, j), []):
                    if what == "xi" and head:
                        copy_xi(k + 1, i)
                    if what == "z":
                        copy_z(k, i)
                    if what == "xproj" and head:
                        copy_dbl(k + 1)
                    if what == "log" and head:
                        if i == 0:
                            nc.scalar.preload_act_table_set(EXP_LN_SET)
                        softplus_log(k + 1, i)
                    if what == "gT" and tail:
                        copy_gT(k + -1, i)
                    if what == "x1T" and tail:
                        copy_x1T(k + -1, i)
                    if what == "tanh" and tail:
                        tanh_gate(k + -1, i)

            def decays(k, q, j, head):
                i = 4 * q + 2 + j
                if i < STEPS:
                    decay_step(k, i)
                elif head:
                    decay_step(k + 1, i - STEPS)

            def evacuations(k, q, j, first):
                if q >= 1:
                    evacuate(k, 4 * (q - 1) + j)
                elif not first:
                    evacuate(k + -1, 60 + j)

            def silu_quads(k, q, tail, head):
                for step in SILU_ORDER:
                    what, i = step
                    if what == "decay":
                        decays(k, q + i // 4, i % 4, head)
                    if what == "hT":
                        evacuations(k, q + i // 4, i % 4, False)
                    if what == "side":
                        side(k, q + i // 4, i % 4, tail, head)
                    if what == "u" and head:
                        silu_u(k + 1, i)
                    if what == "sz":
                        silu_z(k, i)

            def chunk(k, tail, head, first=False):
                q = 0
                while q < QUADS:
                    if q == SILU_QUAD:
                        silu_quads(k, q, tail, head)
                        q += 2
                        continue
                    for j in range(4):
                        decays(k, q, j, head)
                        evacuations(k, q, j, first)
                        side(k, q, j, tail, head)
                    q += 1

            eng.wait_ge(l_w, ALL_LOADED)
            act(a_neg[:, :, :], a_neg[:, :, :], ACT.Exp).then_inc(a_set, 1)
            k0 = Chunk(0, 0)
            for cb in range(CB):
                copy_xi(k0, cb)
            for cb in range(CB):
                silu_u(k0, cb)
            copy_dbl(k0)
            nc.scalar.preload_act_table_set(EXP_LN_SET)
            for half in range(2):
                softplus_log(k0, half)
            eng.wait_ge(v_set, SETUP_V)
            decay_step(k0, 0)
            decay_step(k0, 1)
            for half in range(2):
                chunk(Chunk(0, half), half == 1, True, half == 0)
            with eng.Fori(1, ROWS - 1) as row:
                for half in range(2):
                    chunk(Chunk(row, half), True, True)
            for half in range(2):
                chunk(Chunk(ROWS - 1, half), True, half == 0)
            kl = Chunk(ROWS - 1, 1)
            for g in range(60, 64):
                evacuate(kl, g)
            for cb in range(CB):
                copy_gT(kl, cb)
            for dh in range(DH):
                copy_x1T(kl, dh)
            for m in range(HB):
                tanh_gate(kl, m)

        @block.vector
        def _(eng):
            tt, ts, stt = nc.vector.tensor_tensor, nc.vector.tensor_scalar, nc.vector.scalar_tensor_tensor

            def scan(k, i):
                q = i // 4
                wait(eng, a_da, k.count(STEPS, i + 1))
                if i % 2 == 0:
                    wait(eng, g_dr, k.count(32, i // 2 + 1))
                if i % 4 == 0:
                    wait(eng, p_t, k.count(64, 4 * (q - 1)))
                start = 0.0
                if k.parity:
                    start = state[:, i:i + 1]
                    if i == 0:
                        eng.wait_ge(v_st, k.count(QUADS // 2, QUADS // 2))
                elif i % 4 == 0 and q >= 2:
                    eng.wait_ge(v_st, k.count(QUADS // 2, q - 1))
                nc.vector.tensor_tensor_scan(h[:, q % 2, :, i % 4], decay[decay_bank(k.parity, i)][:, :],
                                             drive[:, (i // 2) % 4, i % 2, :], start, ALU.mult, ALU.add)\
                  .then_inc(v_h, 1)

            def save_state(k, q):
                eng.wait_ge(v_h, k.count(STEPS, 4 * q + 4))
                nc.vector.tensor_copy(state[:, 4 * q:4 * q + 4], h[:, q % 2, T - 1, :]).then_inc(v_st, 1)

            def gate_y(k, cb):
                wait(eng, p_y, k.count(64, 16 * (cb + 1)))
                if cb == 0:
                    wait(eng, a_sz, k.count(4, 4))
                    wait(eng, p_gT, k.count(4, 0))
                cols = slice(cb * P, (cb + 1) * P)
                tt(yg[:, :, cols], yb[:, :].rearrange("p (a c) -> p a c", c=P), sz[:, :, cols], ALU.mult)\
                    .then_inc(v_yg, 1)

            def conv(k, cb, part):
                s = cb % 2
                done = 6 * cb
                if part == 0:
                    wait(eng, v_conv, k.count(24, done))
                    wait(eng, v_dtu, k.count(2, 0))
                    if k.parity:
                        nc.vector.tensor_copy(xi[:, s, 0:KW - 1], hist[:, cb, :]).then_inc(v_conv, 1)
                    else:
                        nc.vector.memset(xi[:, s, 0:KW - 1], 0.0).then_inc(v_conv, 1)
                    wait(eng, a_xi, k.count(4, cb + 1))
                    wait(eng, a_u, k.count(4, 0))
                    eng.wait_ge(v_conv, k.count(24, done + 1))
                    nc.vector.tensor_copy(hist[:, cb, :], xi[:, s, T:T + KW - 1])\
                      .then_inc(v_conv, 1)
                    ts(acc[:, cb, :], xi[:, s, 3:3 + T], cw[:, cb, 3:4], cbias[:, cb:cb + 1],
                       ALU.mult, ALU.add).then_inc(v_conv, 1)
                    taps = (2,)
                else:
                    taps = (1, 0)
                for tap in taps:
                    eng.wait_ge(v_conv, k.count(24, done + 5 - tap))
                    stt(acc[:, cb, :], xi[:, s, tap:tap + T], cw[:, cb, tap:tap + 1], acc[:, cb, :],
                        ALU.mult, ALU.add).then_inc(v_conv, 1)

            def add_bias(k, cb):
                wait(eng, p_dt, k.count(4, cb + 1))
                if cb == 0:
                    wait(eng, a_u, k.count(4, 4))
                ts(acc[:, cb, :], bx[:, :], bdt[:, cb:cb + 1], None, ALU.add).then_inc(v_xb, 1)

            def clamp(k, half):
                eng.wait_ge(v_xb, k.count(4, 2 * half + 2))
                if half == 1:
                    eng.wait_ge(v_dt, k.count(2, 1))
                else:
                    eng.wait_ge(v_conv, k.count(24, 24))
                ts(xi[:, :, 0:T], acc[:, 2 * half:2 * half + 2, :], 40.0, None, ALU.min).then_inc(v_mn, 1)

            def dt_half(k, half):
                two = slice(2 * half, 2 * half + 2)
                wait(eng, a_ln, k.count(2, half + 1))
                wait(eng, a_da, k.count(STEPS, -STEPS + 32 * (half + 1)))
                tt(dt[:, two, :], acc[:, two, :], xi[:, :, 0:T], ALU.max).then_inc(v_dt, 1)
                eng.wait_ge(v_dt, k.count(2, half + 1))
                wait(eng, a_u, k.count(4, 4))
                wait(eng, g_dr, k.count(32, -32 + 16 * (half + 1)))
                tt(dtu[:, two, :], dt[:, two, :], u[:, k.parity, two, :], ALU.mult).then_inc(v_dtu, 1)

            def add_and_stats(k, tb, norm, ready, bank, done, stat):
                wait(eng, ready, k.count(4, tb + 1))
                if norm == 0 and tb == 0:
                    wait(eng, l_res, k.count(16, 16))
                tt(res[:, tb, :], bank[:, 0:DM], res[:, tb, :], ALU.add).then_inc(done, 1)
                eng.wait_ge(done, k.count(4, tb + 1))
                nc.vector.bn_stats(stats[:, norm, tb, :], res[:, tb, :]).then_inc(stat, 1)
                eng.wait_ge(stat, k.count(8, 2 * tb + 1))
                nc.vector.memset(spare[:, :], 0.0)
                nc.vector.bn_aggr(mv[:, norm, tb, :], stats[:, norm, tb, :]).then_inc(stat, 1)

            def normalise(k, norm, done):
                wait(eng, g_n[norm], k.count(2, 2))
                for tb in range(TB):
                    ts(res[:, tb, :], res[:, tb, :], mv[:, norm, tb, 0:1], rstd[:, norm, tb:tb + 1],
                       ALU.subtract, ALU.mult).then_inc(done, 1)

            def gate_silu(k, m):
                wait(eng, a_th, k.count(6, m + 1))
                stt(hid[:, m, :], hid[:, m, :], 1.0, bx[:, :], ALU.add, ALU.mult).then_inc(v_gs, 1)

            def hidden(k, m):
                wait(eng, p_up, k.count(6, m + 1))
                eng.wait_ge(v_gs, k.count(6, m + 1))
                tt(hid[:, m, :], by[:, :], hid[:, m, :], ALU.mult).then_inc(v_hid, 1)

            def side(k, q, j, tail, head, first, late):
                for what, i, *part in DVE_SIDE.get((q, j), []):
                    if what == "dt_half":
                        if i == 1:
                            dt_half(k, 1)
                        elif head:
                            dt_half(k + 1, 0)
                    if what == "conv" and head:
                        conv(k + 1, i, part[0])
                    if what == "gate_y":
                        if i < 3:
                            gate_y(k, i)
                        elif not first:
                            gate_y(k + -1, 3)
                    if what == "xb" and head:
                        add_bias(k + 1, i)
                    if what == "min" and head:
                        clamp(k + 1, i)
                    if what == "r1" and tail:
                        add_and_stats(k + -1, i, 0, p_out, by, v_r1, v_s1)
                    if what == "norm1" and tail:
                        normalise(k + -1, 0, v_x1)
                    if what == "gs" and tail:
                        gate_silu(k + -1, i)
                    if what == "hid" and tail:
                        hidden(k + -1, i)
                    if what == "r2" and tail:
                        add_and_stats(k + -1, i, 1, p_down, (by, bx)[i % 2], v_r2, v_s2)
                    if what == "norm2" and late:
                        normalise(k + -2, 1, v_o)

            def chunk(k, tail, head, first=False, late=True):
                for q in range(QUADS):
                    for j in range(4):
                        scan(k, 4 * q + j)
                        side(k, q, j, tail, head, first, late)
                    if not k.parity:
                        save_state(k, q)

            eng.wait_ge(l_w, ALL_LOADED)
            for w, s in ((w_g, 1.0 / 127.0), (w_u, 1.0 / 127.0)):
                ts(w[:, :, :], w[:, :, :].bitcast(I32), s, None, ALU.mult).then_inc(v_set, 1)
            ts(w_d[:, :, :], w_d[:, :, :].bitcast(I32), 1.0 / 127.0, 0.5, ALU.mult, ALU.mult)\
                .then_inc(v_set, 1)
            eng.wait_ge(g_set, 5)
            for cb in range(CB):
                ts(diag_d[:, cb, :], ident[:, :], dsk[:, cb:cb + 1], None, ALU.mult).then_inc(v_set, 1)
            eng.wait_ge(a_set, 1)
            ts(a_neg[:, :, :], a_neg[:, :, :], -1.0, None, ALU.mult).then_inc(v_set, 1)
            k0 = Chunk(0, 0)
            for cb in range(CB):
                conv(k0, cb, 0)
                conv(k0, cb, 1)
            for cb in range(CB):
                add_bias(k0, cb)
            clamp(k0, 0)
            dt_half(k0, 0)
            clamp(k0, 1)
            for half in range(2):
                chunk(Chunk(0, half), half == 1, True, half == 0, False)
            with eng.Fori(1, ROWS - 1) as row:
                for half in range(2):
                    chunk(Chunk(row, half), True, True)
            for half in range(2):
                chunk(Chunk(ROWS - 1, half), True, half == 0)
            kl = Chunk(ROWS - 1, 1)
            normalise(kl + -1, 1, v_o)
            gate_y(kl, 3)
            for tb in range(TB):
                add_and_stats(kl, tb, 0, p_out, by, v_r1, v_s1)
            normalise(kl, 0, v_x1)
            for m in range(HB):
                gate_silu(kl, m)
                hidden(kl, m)
            for tb in range(TB):
                add_and_stats(kl, tb, 1, p_down, (by, bx)[tb % 2], v_r2, v_s2)
            normalise(kl, 1, v_o)

        @block.tensor
        def _(eng):
            mm = nc.tensor.matmul

            def transposes(k, g):
                q, f = g // 4, g % 4
                if f == 0:
                    wait(eng, v_h, k.count(STEPS, 4 * q + 4))
                wait(eng, a_ev, k.count(64, g - 1))
                for b in range(4):
                    t0 = (4 * f + b) * TS
                    last = nc.tensor.transpose(tp[g % 2][:, b * P:(b + 1) * P],
                                               h[:, q % 2, t0:t0 + TS, :].rearrange("p t s -> p (t s)"), ident[:, :])
                last.then_inc(p_t, 1)

            def skip_term(k, cb):
                wait(eng, v_yg, k.count(4, cb))
                wait(eng, a_u, k.count(4, 4))
                for tb in range(TB):
                    mm(yb[:, tb * P:(tb + 1) * P], u[:, k.parity, cb, tb * P:(tb + 1) * P],
                       diag_d[:, cb, :], start=tb == 0, stop=False, skip_group_check=True)

            def sum_states(k, g):
                q, f = g // 4, g % 4
                if g % 16 == 0:
                    skip_term(k, g // 16)
                if g < 16 and f == 0:
                    wait(eng, g_dc, k.count(4, q + 1))
                wait(eng, a_ev, k.count(64, g + 1))
                for b in range(4):
                    last = mm(yb[b * TS:(b + 1) * TS, f * P:(f + 1) * P], diag_c[:, q % 4, 4 * f + b, :],
                              hT[:, g % 4, b * P:(b + 1) * P], start=False, stop=q % 4 == 3,
                              skip_group_check=True)
                last.then_inc(p_y, 1)

            def product(bank, pairs, done):
                for i, (lhsT, rhs) in enumerate(pairs):
                    last = mm(bank, lhsT, rhs, start=i == 0, stop=i == len(pairs) - 1)
                last.then_inc(done, 1)

            def in_xi(k, cb, tail_before):
                if cb == 0:
                    wait(eng, l_xt[k.parity], k.row * 16 + (k.half // 2 + 1) * 16)
                    if tail_before:
                        wait(eng, v_r2, k.count(4, -8))
                    else:
                        wait(eng, v_xb, k.count(4, 0))
                else:
                    wait(eng, a_xi, k.count(4, cb))
                product(bx[:, :], [(w_in[:, d, cb * P:(cb + 1) * P], xt[:, k.parity, d, :])
                                   for d in range(DH)], p_xi)

            def in_z(k, tb, head):
                if tb == 0 and head:
                    wait(eng, a_xi, k.count(4, 8))
                if tb == 0 and not head:
                    wait(eng, v_r2, k.count(4, -4))
                if tb > 0:
                    wait(eng, a_z, k.count(4, tb))
                product(bx[:, :], [(xt[:, k.parity, d, tb * P:(tb + 1) * P], w_in[:, d, DI:2 * DI])
                                   for d in range(DH)], p_z)

            def x_proj(k, z_before):
                wait(eng, a_z, z_before)
                wait(eng, a_xi, k.count(4, 4))
                wait(eng, a_u, k.count(4, 4))
                product(bx[0:R + 2 * N, :], [(w_x[:, c, :], u[:, k.parity, c, :]) for c in range(CB)], p_x)

            def dt_proj(k, cb):
                if cb == 0:
                    wait(eng, a_dbl, k.count(1, 1))
                else:
                    wait(eng, v_xb, k.count(4, cb))
                product(bx[:, :], [(w_dt[:, cb * P:(cb + 1) * P], dbl[0:R, :])], p_dt)

            def turn_gated(k, cb):
                wait(eng, v_yg, k.count(4, cb + 1))
                if cb == 0:
                    wait(eng, v_r2, k.count(4, -1))
                else:
                    wait(eng, a_gT, k.count(4, cb))
                for tb in range(TB):
                    last = nc.tensor.transpose(by[:, tb * P:(tb + 1) * P],
                                               yg[:, tb, cb * P:(cb + 1) * P], ident[:, :])
                last.then_inc(p_gT, 1)

            def out_proj(k, tb):
                if tb == 0:
                    wait(eng, a_gT, k.count(4, 4))
                else:
                    wait(eng, v_r1, k.count(4, tb))
                product(by[:, 0:DM], [(hid[:, c, tb * P:(tb + 1) * P], w_out[:, c, :])
                                      for c in range(CB)], p_out)

            def turn_x1(k, dh):
                if dh == 0:
                    wait(eng, v_x1, k.count(4, 4))
                else:
                    wait(eng, a_x1T, k.count(2, 1))
                for tb in range(TB):
                    last = nc.tensor.transpose(by[:, tb * P:(tb + 1) * P],
                                               res[:, tb, dh * P:(dh + 1) * P], ident[:, :])
                last.then_inc(p_x1T, 1)

            def gate_up(k, m, weight, bank, done):
                x1 = xt[:, (k.parity + 1) % 2, :, :]
                product(bank[:, :], [(weight[:, d, m * P:(m + 1) * P], x1[:, d, :])
                                     for d in range(DH)], done)

            def gate(k, m, before):
                if m == 0:
                    wait(eng, a_x1T, k.count(2, 2))
                    wait(eng, *before)
                else:
                    wait(eng, v_gs, k.count(6, m))
                gate_up(k, m, w_g, bx, p_gate)

            def up(k, m):
                if m == 0:
                    wait(eng, a_x1T, k.count(2, 2))
                else:
                    wait(eng, v_hid, k.count(6, m))
                gate_up(k, m, w_u, by, p_up)

            def down(k, tb):
                if tb < 2:
                    wait(eng, v_hid, k.count(6, 6))
                else:
                    wait(eng, v_r2, k.count(4, tb - 1))
                product((by, bx)[tb % 2][:, 0:DM], [(hid[:, m, tb * P:(tb + 1) * P], w_d[:, m, :])
                                                    for m in range(HB)], p_down)

            def side(k, q, j, tail, head, tail_before):
                for what, i in PE_SIDE.get((q, j), []):
                    if what == "xi" and head:
                        in_xi(k + 1, i, tail_before)
                    if what == "z":
                        in_z(k, i, head)
                    if what == "xproj" and head:
                        x_proj(k + 1, k.count(4, 4))
                    if what == "dt" and head:
                        dt_proj(k + 1, i)
                    if what == "gT" and tail:
                        turn_gated(k + -1, i)
                    if what == "out" and tail:
                        out_proj(k + -1, i)
                    if what == "x1T" and tail:
                        turn_x1(k + -1, i)
                    if what == "gate" and tail:
                        gate(k + -1, i, (v_xb, (k + 1).count(4, 4)) if head else (a_z, k.count(4, 4)))
                    if what == "up" and tail:
                        up(k + -1, i)
                    if what == "down" and tail:
                        down(k + -1, i)

            def chunk(k, tail, head, first=False, second=False):
                for q in range(QUADS):
                    for j in range(4):
                        g = 4 * (q - 1) + j
                        if g >= 0:
                            transposes(k, g)
                        elif not first:
                            transposes(k + -1, 64 + g)
                        side(k, q, j, tail, head, not (first or second))
                        if g >= 1:
                            sum_states(k, g - 1)
                        elif not first:
                            sum_states(k + -1, 63 + g)

            eng.wait_ge(l_w, ALL_LOADED)
            eng.wait_ge(g_set, 5)
            eng.wait_ge(v_set, SETUP_V)
            k0 = Chunk(0, 0)
            for cb in range(CB):
                in_xi(k0, cb, False)
            x_proj(k0, 0)
            for cb in range(CB):
                dt_proj(k0, cb)
            for half in range(2):
                chunk(Chunk(0, half), half == 1, True, half == 0, half == 1)
            with eng.Fori(1, ROWS - 1) as row:
                for half in range(2):
                    chunk(Chunk(row, half), True, True)
            for half in range(2):
                chunk(Chunk(ROWS - 1, half), True, half == 0)
            kl = Chunk(ROWS - 1, 1)
            for g in range(60, 64):
                transposes(kl, g)
                sum_states(kl, g - 1)
            sum_states(kl, 63)
            for cb in range(CB):
                turn_gated(kl, cb)
            for tb in range(TB):
                out_proj(kl, tb)
            for dh in range(DH):
                turn_x1(kl, dh)
            for m in range(HB):
                gate(kl, m, (v_r2, kl.count(4, 0)))
                up(kl, m)
            for tb in range(TB):
                down(kl, tb)


def kernel(L0_attn_x, L0_attn_W_in, L0_attn_conv_w, L0_attn_conv_b, L0_attn_W_xproj, L0_attn_W_dt,
           L0_attn_b_dt, L0_attn_A_log, L0_attn_D_skip, L0_attn_W_out, L0_ffn_w_gate, L0_ffn_w_up,
           L0_ffn_w_down):
    import numpy as np
    import concourse.bacc as bacc
    from concourse.bass_utils import run_bass_kernel_spmd

    def columns(v):
        return np.asarray(v).reshape(-1, P).T

    x = np.ascontiguousarray(L0_attn_x).reshape(-1, DM)
    arrays = {
        "x": x, "xT": x.T, "W_inT": L0_attn_W_in.T, "conv_w": L0_attn_conv_w, "conv_b": columns(L0_attn_conv_b),
        "W_xT": L0_attn_W_xproj.T, "W_dtT": L0_attn_W_dt.T, "b_dt": columns(L0_attn_b_dt), "A_log": L0_attn_A_log,
        "D_skip": columns(L0_attn_D_skip), "W_outT": L0_attn_W_out.T, "w_gT": L0_ffn_w_gate.T,
        "w_uT": L0_ffn_w_up.T, "w_dT": L0_ffn_w_down.T,
    }
    arrays = {f"in_{k}": np.ascontiguousarray(v) for k, v in arrays.items()}
    nc = bacc.Bacc("TRN2", target_bir_lowering=False, num_devices=1)
    args = [nc.dram_tensor(k, v.shape, mybir.dt.from_np(v.dtype), kind="ExternalInput").ap()
            for k, v in arrays.items()]
    out = nc.dram_tensor("out", x.shape, F32, kind="ExternalOutput").ap()
    mamba_ffn(nc, *args, out)
    got = run_bass_kernel_spmd(nc, [arrays], core_ids=[0]).results[0]["out"]
    return got.reshape(L0_attn_x.shape)
```

```python
from contextlib import ExitStack

import concourse.bass as bass
from concourse import mybir

P = 128
T = 512
TB = T // P
TS = 32
DM = 256
DI = 512
CB = DI // P
N = 16
R = 16
KW = 4
HD = 768
HB = HD // P
DH = DM // P
EPS = 1e-5
QUADS = CB * N // 4
STEPS = CB * N
EXP_LN_SET = "natural_log_exp_and_others"

ALU = mybir.AluOpType
ACT = mybir.ActivationFunctionType
F32 = mybir.dt.float32
I32 = mybir.dt.int32

PE_SIDE = {
    (0, 1): [("xi", 0)], (0, 3): [("xi", 1)], (1, 1): [("xi", 2)], (1, 3): [("xi", 3), ("turn", 3)],
    (2, 1): [("z", 0)], (2, 2): [("z", 1), ("out", 0)], (3, 1): [("z", 2)], (4, 1): [("z", 3)],
    (4, 3): [("out", 1), ("out", 2)], (5, 0): [("out", 3), ("xproj", 0)], (5, 3): [("x1T", 0)],
    (6, 0): [("dt", 0), ("dt", 1)], (6, 1): [("x1T", 1), ("dt", 2), ("dt", 3)], (6, 3): [("turn", 0)],
    (7, 1): [("gate", 0)], (7, 2): [("up", 0)], (8, 1): [("gate", 1)], (8, 3): [("up", 1)],
    (9, 1): [("gate", 2)], (9, 3): [("up", 2)], (10, 0): [("turn", 1)], (10, 1): [("up", 3)],
    (10, 2): [("gate", 3)], (11, 2): [("gate", 4)], (11, 3): [("up", 4)], (12, 1): [("gate", 5)],
    (12, 2): [("up", 5)], (13, 2): [("down", 0)], (13, 3): [("turn", 2), ("down", 1)],
    (14, 3): [("down", 2)], (15, 1): [("down", 3)],
}
ACT_SIDE = {
    (0, 1): [("xi", 0)], (0, 3): [("xi", 1)], (1, 0): [("y", 3)], (1, 1): [("xi", 2)],
    (2, 0): [("xi", 3)], (2, 1): [("z", 0)], (2, 2): [("z", 1)], (4, 0): [("z", 2)], (4, 1): [("z", 3)],
    (5, 0): [("y", 0)], (5, 2): [("xproj", 0)], (6, 0): [("x1T", 0)], (6, 1): [("x1T", 1)],
    (7, 2): [("tanh", 0)], (8, 2): [("tanh", 1)], (9, 0): [("y", 1)], (9, 3): [("tanh", 2)],
    (10, 2): [("tanh", 3)], (11, 2): [("tanh", 4)], (12, 2): [("tanh", 5)],
    (13, 0): [("y", 2), ("log", 0)], (14, 2): [("log", 1)],
}
SILU_QUAD = 4
SILU_ORDER = [
    ("side", 0), ("decay", 0), ("hT", 0), ("decay", 1), ("hT", 1), ("decay", 2), ("side", 1),
    ("decay", 3), ("side", 2), ("side", 3), ("u", 0), ("u", 1), ("hT", 2), ("u", 2), ("u", 3), ("hT", 3),
    ("sz", 0), ("hT", 4), ("sz", 1), ("sz", 2), ("sz", 3), ("decay", 4), ("side", 4), ("hT", 5),
    ("decay", 5), ("side", 5), ("hT", 6), ("side", 6), ("decay", 6), ("hT", 7), ("side", 7), ("decay", 7),
]
DVE_SIDE = {
    (0, 0): [("dt_half", 1)], (0, 2): [("conv", 0, 0)], (0, 3): [("conv", 0, 1)],
    (1, 0): [("conv", 1, 0)], (1, 2): [("conv", 1, 1)],
    (1, 3): [("conv", 2, 0), ("norm2", 0), ("conv", 2, 1)], (2, 0): [("skip", 3), ("conv", 3, 0)],
    (2, 1): [("conv", 3, 1)], (2, 3): [("r1", 0)], (4, 3): [("r1", 1), ("r1", 2)], (5, 0): [("r1", 3)],
    (5, 1): [("norm1", 0)], (6, 1): [("xb", 0), ("xb", 1)], (6, 3): [("xb", 2)], (7, 0): [("xb", 3)],
    (7, 1): [("skip", 0), ("min", 0)], (7, 3): [("gs", 0)], (8, 1): [("hid", 0)], (8, 3): [("gs", 1)],
    (9, 1): [("hid", 1)], (9, 3): [("gs", 2), ("hid", 2)], (10, 1): [("skip", 1)], (10, 3): [("gs", 3)],
    (11, 3): [("gs", 4)], (12, 0): [("hid", 3), ("hid", 4)], (12, 2): [("gs", 5)], (13, 0): [("hid", 5)],
    (13, 2): [("dt_half", 0)], (13, 3): [("r2", 0), ("min", 1)], (14, 0): [("skip", 2)],
    (14, 2): [("r2", 1)], (15, 3): [("r2", 2), ("r2", 3)],
}
POOL_GATE = {2: 3, 8: 0, 11: 1, 15: 2}
POOL_NORM = {0: 1, 6: 0}


class Chunk:

    def __init__(self, row, half):
        self.row, self.half = row, half

    def __add__(self, d):
        return Chunk(self.row, self.half + d)

    @property
    def parity(self):
        return self.half % 2

    def count(self, per, i):
        return self.row * (2 * per) + (self.half * per + i)

    def tokens(self):
        return self.row * (2 * T) + self.half * T


def wait(eng, sem, value):
    if not isinstance(value, int) or value > 0:
        eng.wait_ge(sem, value)


def decay_slot(parity, i):
    return (i + parity) % 3


def decay_before(parity, i):
    if i >= 3:
        return i - 3
    slot = decay_slot(parity, i)
    return max(j for j in range(STEPS) if decay_slot(1 - parity, j) == slot) - STEPS


def mamba_ffn(nc, x, xT, W_inT, conv_w, conv_b, W_xT, W_dtT, b_dt, A_log, D_skip, W_outT,
              w_gT, w_uT, w_dT, out):
    ROWS = x.shape[0] // (2 * T)
    bc_dram = nc.dram_tensor("bc_scratch", [2 * N, T], F32, kind="Internal").ap()
    with ExitStack() as ctx:
        def sb(name, shape, dt=F32):
            return ctx.enter_context(nc.sbuf_tensor(name, shape, dt))

        def pb(name):
            return ctx.enter_context(nc.psum_tensor(name, [P, 512], F32))

        def sem(name):
            return ctx.enter_context(nc.semaphore(name))

        w_in = sb("w_in", [P, DH, 2 * DI])
        w_x = sb("w_x", [P, CB, R + 2 * N])
        w_dt = sb("w_dt", [R, DI])
        w_out = sb("w_out", [P, CB, DM])
        w_g = sb("w_g", [P, DH, HD])
        w_u = sb("w_u", [P, DH, HD])
        w_d = sb("w_d", [P, HB, DM])
        cw = sb("cw", [P, CB, KW])
        cbias = sb("cbias", [P, CB])
        bdt = sb("bdt", [P, CB])
        dsk = sb("dsk", [P, CB])
        a_neg = sb("a_neg", [P, CB, N])
        ident = sb("ident", [P, P])
        of_token = sb("of_token", [P, TS])
        half_neg = sb("half_neg", [P, TB])
        eps = sb("eps", [P, TB])
        spare = sb("spare", [P, 1])
        xt = sb("xt", [P, 2, DH, T])
        res = sb("res", [P, TB, DM])
        xi = sb("xi", [P, 2, KW - 1 + T])
        hist = sb("hist", [P, CB, KW - 1])
        acc = sb("acc", [P, CB, T])
        u = sb("u", [P, 2, CB, T])
        dt = sb("dt", [P, CB, T])
        dtu = sb("dtu", [P, CB, T])
        sz = sb("sz", [P, CB, T])
        b_all = sb("b_all", [P, N, T])
        c_col = sb("c_col", [P, 4, N])
        diag_c = sb("diag_c", [P, 4, N, TS])
        dbl = sb("dbl", [R + 2 * N, T])
        drive = sb("drive", [P, 4, 2, T])
        h = sb("h", [P, 2, T, 4])
        state = sb("state", [P, STEPS])
        hT = sb("hT", [P, 2, T])
        decay = sb("decay", [P, 3, T])
        yt = sb("yt", [P, T])
        yg = sb("yg", [P, CB, T])
        hid = sb("hid", [P, HB, T])
        stats = sb("stats", [P, 2, TB, 6])
        mv = sb("mv", [P, 2, TB, 2])
        var = sb("var", [P, 2, TB])
        rstd = sb("rstd", [P, 2, TB])
        tp = [pb(f"tp{i}") for i in range(2)]
        yb = [pb(f"yb{i}") for i in range(2)]
        bx = [pb(f"bx{i}") for i in range(2)]
        by = [pb(f"by{i}") for i in range(2)]
        xi_bank = z_bank = lambda i: bx[i % 2]
        xproj_bank = bx[0]
        dt_bank = gate_bank = lambda i: bx[(i + 1) % 2]
        turn_bank = lambda cb: by[cb < CB - 1]
        out_bank = x1T_bank = lambda i: by[(i + 1) % 2]
        up_bank = lambda m: by[(m + m // 3) % 2]
        down_bank = lambda tb: (bx[1], by[0], bx[0], by[1])[tb]

        l_in = sem("l_in"); l_cv = sem("l_cv"); l_w = sem("l_w"); l_xt = [sem("l_xt0"), sem("l_xt1")]; l_res = sem("l_res")
        st_bc = sem("st_bc"); l_c = sem("l_c"); l_b = [sem(f"l_b{g}") for g in range(4)]
        st_out = sem("st_out")
        p_t = sem("p_t"); p_y = sem("p_y"); p_xi = sem("p_xi"); p_z = sem("p_z"); p_x = sem("p_x")
        p_dt = sem("p_dt"); p_turn = sem("p_turn"); p_out = sem("p_out"); p_x1T = sem("p_x1T")
        p_gate = sem("p_gate"); p_up = sem("p_up"); p_down = sem("p_down")
        a_da = sem("a_da"); a_ev = sem("a_ev"); a_xi = sem("a_xi"); a_u = sem("a_u"); a_z = sem("a_z")
        a_sz = sem("a_sz"); a_dbl = sem("a_dbl"); a_e = sem("a_e"); a_ln = sem("a_ln")
        a_y = sem("a_y"); a_x1T = sem("a_x1T"); a_th = sem("a_th"); a_set = sem("a_set")
        v_h = sem("v_h"); v_st = sem("v_st"); v_y = sem("v_y"); v_conv = sem("v_conv")
        v_xb = sem("v_xb"); v_mn = sem("v_mn"); v_dt = sem("v_dt"); v_dtu = sem("v_dtu")
        v_r1 = sem("v_r1"); v_s1 = sem("v_s1"); v_x1 = sem("v_x1"); v_gs = sem("v_gs")
        v_hid = sem("v_hid"); v_r2 = sem("v_r2"); v_s2 = sem("v_s2"); v_o = sem("v_o")
        v_set = sem("v_set")
        g_set = sem("g_set"); g_dr = sem("g_dr"); g_dc = sem("g_dc"); g_y = sem("g_y")
        g_n = [sem("g_n1"), sem("g_n2")]

        conv_loads = [
            (cw[:, :, :], conv_w.rearrange("(a p) n -> p a n", p=P)),
            (cbias[:, :], conv_b),
        ]
        loads = [
            (w_x[:, :, :], W_xT.rearrange("(a p) n -> p a n", p=P)),
            (w_dt[:, :], W_dtT),
            (bdt[:, :], b_dt),
            (a_neg[:, :, :], A_log.rearrange("(a p) n -> p a n", p=P)),
            (dsk[:, :], D_skip),
            (w_out[:, :, :], W_outT.rearrange("(a p) n -> p a n", p=P)),
            (w_g[:, :, :].bitcast(I32), w_gT.rearrange("(a p) n -> p a n", p=P)),
            (w_u[:, :, :].bitcast(I32), w_uT.rearrange("(a p) n -> p a n", p=P)),
            (w_d[:, :, :].bitcast(I32), w_dT.rearrange("(a p) n -> p a n", p=P)),
        ]
        ALL_LOADED = 16 * (1 + len(loads))
        SETUP_V = 4

        block = ctx.enter_context(nc.Block())

        @block.sync
        def _(eng):
            def load_xt(k):
                eng.dma_start(xt[:, k.parity, :, :],
                              xT[:, bass.ds(k.tokens(), T)].rearrange("(a p) t -> p a t", p=P))\
                   .then_inc(l_xt[k.parity], 16)

            def spread_bc(k, b_first=False):
                wait(eng, a_dbl, k.count(2, 2))
                eng.dma_start(bc_dram, dbl[R:R + 2 * N, :]).then_inc(st_bc, 16)
                wait(eng, st_bc, k.count(16, 16))
                if b_first:
                    for g in range(4):
                        load_b(g)
                for n in range(N):
                    g, s = n // 4, n % 4
                    eng.dma_start(c_col[s:P - 3 + s:4, g, :], bc_dram[N + n, :].rearrange("(b t) -> t b", t=TS),
                                  allow_slow_non_contiguous=True).then_inc(l_c, 16)

            def load_b(g):
                src = bc_dram[4 * g:4 * g + 4, :].rearrange("(o n) t -> o n t", o=1)
                eng.dma_start(b_all[:, 4 * g:4 * g + 4, :], src.to_broadcast([P, 4, T]))\
                   .then_inc(l_b[g], 16)

            def store(k):
                wait(eng, v_o, k.count(4, 4))
                eng.dma_start(out[bass.ds(k.tokens(), T), :].rearrange("(a p) d -> p a d", p=P),
                              res[:, :, :]).then_inc(st_out, 16)

            def load_res(k):
                wait(eng, st_out, k.count(16, 0))
                eng.dma_start(res[:, :, :],
                              x[bass.ds(k.tokens(), T), :].rearrange("(a p) d -> p a d", p=P))\
                   .then_inc(l_res, 16)

            def chunk(k, tail, head, more, late=True):
                if late:
                    store(k + -2)
                if tail:
                    load_res(k + -1)
                if head:
                    spread_bc(k + 1)
                if more:
                    if tail:
                        wait(eng, p_up, k.count(6, 0))
                    else:
                        wait(eng, p_z, k.count(4, 4))
                    load_xt(k + 2)
                if head:
                    for g in range(4):
                        wait(eng, g_dr, k.count(32, 24 + 2 * g + 2))
                        load_b(g)

            load_xt(Chunk(0, 0))
            for half in (slice(0, DI), slice(DI, 2 * DI)):
                eng.dma_start(w_in[:, :, half], W_inT[:, half].rearrange("(a p) n -> p a n", p=P))\
                   .then_inc(l_in if half.start == 0 else l_w, 16)
                if half.start == 0:
                    for dst, src in conv_loads:
                        eng.dma_start(dst, src).then_inc(l_cv, 16)
            for dst, src in loads:
                eng.dma_start(dst, src).then_inc(l_w, 16)
            load_xt(Chunk(0, 1))
            spread_bc(Chunk(0, 0), b_first=True)
            for half in range(2):
                chunk(Chunk(0, half), half == 1, True, True, False)
            with eng.Fori(1, ROWS - 1) as row:
                for half in range(2):
                    chunk(Chunk(row, half), True, True, True)
            for half in range(2):
                chunk(Chunk(ROWS - 1, half), True, half == 0, False)
            kl = Chunk(ROWS - 1, 1)
            store(kl + -1)
            load_res(kl)
            store(kl)
            eng.wait_ge(st_out, 2 * ROWS * 16)

        @block.gpsimd
        def _(eng):
            def drive_unit(k, j):
                cb, n = j // 8, 2 * (j % 8)
                wait(eng, v_h, k.count(STEPS, 2 * (j - 4) + 2))
                if cb == 0 and n % 4 == 0:
                    wait(eng, l_b[n // 4], k.count(16, 16))
                if j % 16 == 0:
                    wait(eng, v_dtu, k.count(2, j // 16 + 1))
                src = dtu[:, cb, :].rearrange("p (o t) -> p o t", o=1).to_broadcast([P, 2, T])
                nc.gpsimd.tensor_tensor(drive[:, j % 4, :, :], src, b_all[:, n:n + 2, :],
                                        ALU.mult).then_inc(g_dr, 1)

            def diagonals(k, g):
                if g == 0:
                    wait(eng, l_c, k.count(16 * N, 16 * N))
                wait(eng, p_y, k.count(64, -64 + 4 * (12 + g) + 4))
                mask = of_token[:, :].rearrange("p (o t) -> p o t", o=1).to_broadcast([P, N, TS])
                col = c_col[:, g, :].rearrange("p (b o) -> p b o", o=1).to_broadcast([P, N, TS])
                nc.gpsimd.tensor_tensor(diag_c[:, g, :, :], mask, col, ALU.mult).then_inc(g_dc, 1)

            def gate_y(k, cb):
                wait(eng, v_y, k.count(4, cb + 1))
                wait(eng, a_sz, k.count(4, cb + 1))
                nc.gpsimd.tensor_tensor(yg[:, cb, :], yg[:, cb, :], sz[:, cb, :], ALU.mult).then_inc(g_y, 1)

            def inverse_std(k, norm):
                wait(eng, (v_s1, v_s2)[norm], k.count(8, 8))
                nc.gpsimd.tensor_tensor(var[:, norm, :], mv[:, norm, :, 1], eps[:, :], ALU.add)\
                  .then_inc(g_n[norm], 1)
                eng.wait_ge(g_n[norm], k.count(2, 1))
                nc.gpsimd.tensor_tensor(rstd[:, norm, :], var[:, norm, :], half_neg[:, :], ALU.pow)\
                  .then_inc(g_n[norm], 1)

            def chunk(k, tail, head, late=True, first=False):
                for q in range(QUADS):
                    drive_unit(k, 2 * q)
                    drive_unit(k, 2 * q + 1)
                    if q == 1 and first:
                        for g in range(3):
                            diagonals(k, g)
                    if q in POOL_GATE:
                        cb = POOL_GATE[q]
                        if cb < CB - 1:
                            gate_y(k, cb)
                        elif not first:
                            gate_y(k + -1, cb)
                    if POOL_NORM.get(q) == 1 and late:
                        inverse_std(k + -2, 1)
                    if POOL_NORM.get(q) == 0 and tail:
                        inverse_std(k + -1, 0)
                    if q in ((2,) if first else (0, 1)):
                        diagonals(k, 3 if first else q + 2)
                    if q in (14, 15) and head:
                        diagonals(k + 1, q - 14)

            nc.gpsimd.memset(ident[:, :], 0.0).then_inc(g_set, 1)
            nc.gpsimd.memset(half_neg[:, :], -0.5).then_inc(g_set, 1)
            nc.gpsimd.memset(eps[:, :], EPS).then_inc(g_set, 1)
            nc.gpsimd.memset(of_token[:, :], 1.0).then_inc(g_set, 1)
            eng.wait_ge(g_set, 4)
            nc.gpsimd.affine_select(out=ident[:, :], in_=ident[:, :], compare_op=ALU.not_equal, fill=1.0,
                                    base=0, pattern=[[-1, P]], channel_multiplier=1).then_inc(g_set, 1)
            eng.wait_ge(g_set, 5)
            for base, sign in ((0, 1), (3, -1)):
                nc.gpsimd.affine_select(out=of_token[:, :], in_=of_token[:, :], compare_op=ALU.is_ge,
                                        fill=0.0, base=base, pattern=[[-4 * sign, TS]],
                                        channel_multiplier=sign).then_inc(g_set, 1)
                eng.wait_ge(g_set, 6 if sign > 0 else 7)
            for half in range(2):
                chunk(Chunk(0, half), half == 1, True, False, half == 0)
            with eng.Fori(1, ROWS - 1) as row:
                for half in range(2):
                    chunk(Chunk(row, half), True, True)
            for half in range(2):
                chunk(Chunk(ROWS - 1, half), True, half == 0)
            inverse_std(Chunk(ROWS - 1, 0), 1)
            gate_y(Chunk(ROWS - 1, 1), CB - 1)
            inverse_std(Chunk(ROWS - 1, 1), 0)
            inverse_std(Chunk(ROWS - 1, 1), 1)

        @block.scalar
        def _(eng):
            act = nc.scalar.activation

            def decay_step(k, i):
                cb, n = i // N, i % N
                wait(eng, v_h, k.count(STEPS, decay_before(k.parity, i) + 1))
                if i % 32 == 0:
                    wait(eng, v_dt, k.count(2, i // 32 + 1))
                act(decay[:, decay_slot(k.parity, i), :], dt[:, cb, :], ACT.Exp,
                    scale=a_neg[:, cb, n:n + 1]).then_inc(a_da, 1)

            def evacuate(k, g):
                wait(eng, p_t, k.count(64, g + 1))
                wait(eng, p_y, k.count(64, g - 1))
                act(hT[:, g % 2, :], tp[g % 2][:, :], ACT.Copy).then_inc(a_ev, 1)

            def copy_xi(k, cb):
                wait(eng, p_xi, k.count(4, cb + 1))
                if cb >= 2:
                    wait(eng, v_conv, k.count(20, 5 * (cb - 1)))
                else:
                    wait(eng, v_dtu, k.count(2, 0))
                wait(eng, a_u, k.count(4, 0))
                act(acc[:, cb, :], xi_bank(cb)[:, :], ACT.Identity, scale=cw[:, cb, KW - 1:KW],
                    bias=cbias[:, cb:cb + 1]).then_inc(a_xi, 1)
                act(xi[:, cb % 2, KW - 1:], xi_bank(cb)[:, :], ACT.Copy).then_inc(a_xi, 1)

            def copy_z(k, cb):
                wait(eng, p_z, k.count(4, cb + 1))
                wait(eng, g_y, k.count(4, cb - 3))
                act(sz[:, cb, :], z_bank(cb)[:, :], ACT.Copy).then_inc(a_z, 1)

            def copy_y(k, cb):
                wait(eng, p_y, k.count(64, 16 * (cb + 1)))
                wait(eng, p_turn, k.count(4, cb))
                act(yt[:, :], yb[cb % 2][:, :], ACT.Copy).then_inc(a_y, 1)

            def silu_u(k, cb):
                wait(eng, v_conv, k.count(20, 5 * (cb + 1)))
                wait(eng, v_y, k.count(4, -4))
                act(u[:, k.parity, cb, :], acc[:, cb, :], ACT.Silu).then_inc(a_u, 1)

            def silu_z(k, cb):
                eng.wait_ge(a_z, k.count(4, cb + 1))
                act(sz[:, cb, :], sz[:, cb, :], ACT.Silu).then_inc(a_sz, 1)

            def copy_dbl(k):
                wait(eng, p_x, k.count(1, 1))
                wait(eng, st_bc, k.count(16, 0))
                for b in range(2):
                    act(dbl[:, b * T // 2:(b + 1) * T // 2], xproj_bank[b * P // 2:b * P // 2 + R + 2 * N, 0:T // 2],
                        ACT.Copy).then_inc(a_dbl, 1)

            def softplus_log(k, half):
                tmp = xi[:, :, 0:T]
                wait(eng, v_mn, k.count(2, half + 1))
                act(tmp, tmp, ACT.Exp).then_inc(a_e, 1)
                eng.wait_ge(a_e, k.count(2, half + 1))
                act(tmp, tmp, ACT.Ln, bias=1.0).then_inc(a_ln, 1)

            def copy_x1T(k, dh):
                wait(eng, p_x1T, k.count(2, dh + 1))
                act(xt[:, (k.parity + 1) % 2, dh, :], x1T_bank(dh)[:, :], ACT.Copy).then_inc(a_x1T, 1)

            def tanh_gate(k, m):
                wait(eng, p_gate, k.count(6, m + 1))
                act(hid[:, m, :], gate_bank(m)[:, :], ACT.Tanh, scale=0.5).then_inc(a_th, 1)

            def side(k, q, j, tail, head, first):
                for what, i in ACT_SIDE.get((q, j), []):
                    if what == "xi" and head:
                        copy_xi(k + 1, i)
                    if what == "z":
                        copy_z(k, i)
                    if what == "xproj" and head:
                        copy_dbl(k + 1)
                    if what == "log" and head:
                        if i == 0:
                            nc.scalar.preload_act_table_set(EXP_LN_SET)
                        softplus_log(k + 1, i)
                    if what == "y":
                        if i < CB - 1:
                            copy_y(k, i)
                        elif not first:
                            copy_y(k + -1, i)
                    if what == "x1T" and tail:
                        copy_x1T(k + -1, i)
                    if what == "tanh" and tail:
                        tanh_gate(k + -1, i)

            def decays(k, q, j, head):
                i = 4 * q + 2 + j
                if i < STEPS:
                    decay_step(k, i)
                elif head:
                    decay_step(k + 1, i - STEPS)

            def evacuations(k, q, j, first):
                if q >= 1:
                    evacuate(k, 4 * (q - 1) + j)
                elif not first:
                    evacuate(k + -1, 60 + j)

            def silu_quads(k, q, tail, head):
                for step in SILU_ORDER:
                    what, i = step
                    if what == "decay":
                        decays(k, q + i // 4, i % 4, head)
                    if what == "hT":
                        evacuations(k, q + i // 4, i % 4, False)
                    if what == "side":
                        side(k, q + i // 4, i % 4, tail, head, False)
                    if what == "u" and head:
                        silu_u(k + 1, i)
                    if what == "sz":
                        silu_z(k, i)

            def chunk(k, tail, head, first=False):
                q = 0
                while q < QUADS:
                    if q == SILU_QUAD:
                        silu_quads(k, q, tail, head)
                        q += 2
                        continue
                    for j in range(4):
                        decays(k, q, j, head)
                        evacuations(k, q, j, first)
                        side(k, q, j, tail, head, first)
                    q += 1

            k0 = Chunk(0, 0)
            eng.wait_ge(l_cv, 16 * len(conv_loads))
            for cb in range(CB):
                copy_xi(k0, cb)
            for cb in range(CB):
                silu_u(k0, cb)
            copy_dbl(k0)
            nc.scalar.preload_act_table_set(EXP_LN_SET)
            eng.wait_ge(l_w, ALL_LOADED)
            act(a_neg[:, :, :], a_neg[:, :, :], ACT.Exp).then_inc(a_set, 1)
            softplus_log(k0, 0)
            eng.wait_ge(v_set, SETUP_V)
            decay_step(k0, 0)
            decay_step(k0, 1)
            softplus_log(k0, 1)
            for half in range(2):
                chunk(Chunk(0, half), half == 1, True, half == 0)
            with eng.Fori(1, ROWS - 1) as row:
                for half in range(2):
                    chunk(Chunk(row, half), True, True)
            for half in range(2):
                chunk(Chunk(ROWS - 1, half), True, half == 0)
            kl = Chunk(ROWS - 1, 1)
            for g in range(60, 64):
                evacuate(kl, g)
            copy_y(kl, CB - 1)
            for dh in range(DH):
                copy_x1T(kl, dh)
            for m in range(HB):
                tanh_gate(kl, m)

        @block.vector
        def _(eng):
            tt, ts, stt = nc.vector.tensor_tensor, nc.vector.tensor_scalar, nc.vector.scalar_tensor_tensor

            def scan(k, i):
                q = i // 4
                wait(eng, a_da, k.count(STEPS, i + 1))
                if i % 2 == 0:
                    wait(eng, g_dr, k.count(32, i // 2 + 1))
                if i % 4 == 0:
                    wait(eng, p_t, k.count(64, 4 * (q - 1)))
                start = 0.0
                if k.parity:
                    start = state[:, i:i + 1]
                    if i == 0:
                        eng.wait_ge(v_st, k.count(QUADS // 2, QUADS // 2))
                elif i % 4 == 0 and q >= 2:
                    eng.wait_ge(v_st, k.count(QUADS // 2, q - 1))
                nc.vector.tensor_tensor_scan(h[:, q % 2, :, i % 4], decay[:, decay_slot(k.parity, i), :],
                                             drive[:, (i // 2) % 4, i % 2, :], start, ALU.mult, ALU.add)\
                  .then_inc(v_h, 1)

            def save_state(k, q):
                eng.wait_ge(v_h, k.count(STEPS, 4 * q + 4))
                nc.vector.tensor_copy(state[:, 4 * q:4 * q + 4], h[:, q % 2, T - 1, :]).then_inc(v_st, 1)

            def add_skip(k, cb):
                wait(eng, p_turn, k.count(4, cb + 1))
                if cb == 0:
                    wait(eng, p_out, k.count(4, 0))
                    wait(eng, a_u, k.count(4, 4))
                stt(yg[:, cb, :], u[:, k.parity, cb, :], dsk[:, cb:cb + 1], turn_bank(cb)[:, :], ALU.mult, ALU.add)\
                    .then_inc(v_y, 1)

            def conv(k, cb, part):
                s = cb % 2
                done = 5 * cb
                if part == 0:
                    wait(eng, v_conv, k.count(20, done))
                    wait(eng, v_dtu, k.count(2, 0))
                    if k.parity:
                        nc.vector.tensor_copy(xi[:, s, 0:KW - 1], hist[:, cb, :]).then_inc(v_conv, 1)
                    else:
                        nc.vector.memset(xi[:, s, 0:KW - 1], 0.0).then_inc(v_conv, 1)
                    wait(eng, a_xi, k.count(8, 2 * cb + 2))
                    eng.wait_ge(v_conv, k.count(20, done + 1))
                    nc.vector.tensor_copy(hist[:, cb, :], xi[:, s, T:T + KW - 1])\
                      .then_inc(v_conv, 1)
                for tap in ((2,), (1, 0))[part]:
                    eng.wait_ge(v_conv, k.count(20, done + 4 - tap))
                    stt(acc[:, cb, :], xi[:, s, tap:tap + T], cw[:, cb, tap:tap + 1], acc[:, cb, :],
                        ALU.mult, ALU.add).then_inc(v_conv, 1)

            def add_bias(k, cb):
                wait(eng, p_dt, k.count(4, cb + 1))
                if cb == 0:
                    wait(eng, a_u, k.count(4, 4))
                ts(acc[:, cb, :], dt_bank(cb)[:, :], bdt[:, cb:cb + 1], None, ALU.add).then_inc(v_xb, 1)

            def clamp(k, half):
                eng.wait_ge(v_xb, k.count(4, 2 * half + 2))
                if half == 1:
                    eng.wait_ge(v_dt, k.count(2, 1))
                else:
                    eng.wait_ge(v_conv, k.count(20, 20))
                ts(xi[:, :, 0:T], acc[:, 2 * half:2 * half + 2, :], 40.0, None, ALU.min).then_inc(v_mn, 1)

            def dt_half(k, half):
                two = slice(2 * half, 2 * half + 2)
                wait(eng, a_ln, k.count(2, half + 1))
                wait(eng, a_da, k.count(STEPS, -STEPS + 32 * (half + 1)))
                tt(dt[:, two, :], acc[:, two, :], xi[:, :, 0:T], ALU.max).then_inc(v_dt, 1)
                eng.wait_ge(v_dt, k.count(2, half + 1))
                wait(eng, a_u, k.count(4, 4))
                wait(eng, g_dr, k.count(32, -32 + 16 * (half + 1)))
                tt(dtu[:, two, :], dt[:, two, :], u[:, k.parity, two, :], ALU.mult).then_inc(v_dtu, 1)

            def add_and_stats(k, tb, norm, ready, bank, done, stat):
                wait(eng, ready, k.count(4, tb + 1))
                if norm == 0 and tb == 0:
                    wait(eng, l_res, k.count(16, 16))
                tt(res[:, tb, :], bank(tb)[:, 0:DM], res[:, tb, :], ALU.add).then_inc(done, 1)
                eng.wait_ge(done, k.count(4, tb + 1))
                nc.vector.bn_stats(stats[:, norm, tb, :], res[:, tb, :]).then_inc(stat, 1)
                eng.wait_ge(stat, k.count(8, 2 * tb + 1))
                nc.vector.memset(spare[:, :], 0.0)
                nc.vector.bn_aggr(mv[:, norm, tb, :], stats[:, norm, tb, :]).then_inc(stat, 1)

            def normalise(k, norm, done):
                wait(eng, g_n[norm], k.count(2, 2))
                for tb in range(TB):
                    ts(res[:, tb, :], res[:, tb, :], mv[:, norm, tb, 0:1], rstd[:, norm, tb:tb + 1],
                       ALU.subtract, ALU.mult).then_inc(done, 1)

            def gate_silu(k, m):
                wait(eng, a_th, k.count(6, m + 1))
                stt(hid[:, m, :], hid[:, m, :], 1.0, gate_bank(m)[:, :], ALU.add, ALU.mult).then_inc(v_gs, 1)

            def hidden(k, m):
                wait(eng, p_up, k.count(6, m + 1))
                eng.wait_ge(v_gs, k.count(6, m + 1))
                tt(hid[:, m, :], up_bank(m)[:, :], hid[:, m, :], ALU.mult).then_inc(v_hid, 1)

            def side(k, q, j, tail, head, first, late):
                for what, i, *part in DVE_SIDE.get((q, j), []):
                    if what == "dt_half":
                        if i == 1:
                            dt_half(k, 1)
                        elif head:
                            dt_half(k + 1, 0)
                    if what == "conv" and head:
                        conv(k + 1, i, part[0])
                    if what == "skip":
                        if i < CB - 1:
                            add_skip(k, i)
                        elif not first:
                            add_skip(k + -1, i)
                    if what == "xb" and head:
                        add_bias(k + 1, i)
                    if what == "min" and head:
                        clamp(k + 1, i)
                    if what == "r1" and tail:
                        add_and_stats(k + -1, i, 0, p_out, out_bank, v_r1, v_s1)
                    if what == "norm1" and tail:
                        normalise(k + -1, 0, v_x1)
                    if what == "gs" and tail:
                        gate_silu(k + -1, i)
                    if what == "hid" and tail:
                        hidden(k + -1, i)
                    if what == "r2" and tail:
                        add_and_stats(k + -1, i, 1, p_down, down_bank, v_r2, v_s2)
                    if what == "norm2" and late:
                        normalise(k + -2, 1, v_o)

            def chunk(k, tail, head, first=False, late=True):
                for q in range(QUADS):
                    for j in range(4):
                        scan(k, 4 * q + j)
                        side(k, q, j, tail, head, first, late)
                    if not k.parity:
                        save_state(k, q)

            k0 = Chunk(0, 0)
            eng.wait_ge(l_cv, 16 * len(conv_loads))
            for cb in range(CB):
                conv(k0, cb, 0)
                conv(k0, cb, 1)
            eng.wait_ge(l_w, ALL_LOADED)
            for w, s in ((w_g, 1.0 / 127.0), (w_u, 1.0 / 127.0)):
                ts(w[:, :, :], w[:, :, :].bitcast(I32), s, None, ALU.mult).then_inc(v_set, 1)
            ts(w_d[:, :, :], w_d[:, :, :].bitcast(I32), 1.0 / 127.0, 0.5, ALU.mult, ALU.mult)\
                .then_inc(v_set, 1)
            eng.wait_ge(a_set, 1)
            ts(a_neg[:, :, :], a_neg[:, :, :], -1.0, None, ALU.mult).then_inc(v_set, 1)
            for cb in range(CB):
                add_bias(k0, cb)
            clamp(k0, 0)
            dt_half(k0, 0)
            clamp(k0, 1)
            for half in range(2):
                chunk(Chunk(0, half), half == 1, True, half == 0, False)
            with eng.Fori(1, ROWS - 1) as row:
                for half in range(2):
                    chunk(Chunk(row, half), True, True)
            for half in range(2):
                chunk(Chunk(ROWS - 1, half), True, half == 0)
            kl = Chunk(ROWS - 1, 1)
            normalise(kl + -1, 1, v_o)
            add_skip(kl, CB - 1)
            for tb in range(TB):
                add_and_stats(kl, tb, 0, p_out, out_bank, v_r1, v_s1)
            normalise(kl, 0, v_x1)
            for m in range(HB):
                gate_silu(kl, m)
                hidden(kl, m)
            for tb in range(TB):
                add_and_stats(kl, tb, 1, p_down, down_bank, v_r2, v_s2)
            normalise(kl, 1, v_o)

        @block.tensor
        def _(eng):
            mm = nc.tensor.matmul

            def transposes(k, g):
                q, f = g // 4, g % 4
                if f == 0:
                    wait(eng, v_h, k.count(STEPS, 4 * q + 4))
                wait(eng, a_ev, k.count(64, g - 1))
                for b in range(4):
                    t0 = (4 * f + b) * TS
                    last = nc.tensor.transpose(tp[g % 2][:, b * P:(b + 1) * P],
                                               h[:, q % 2, t0:t0 + TS, :].rearrange("p t s -> p (t s)"), ident[:, :])
                last.then_inc(p_t, 1)

            def sum_states(k, g):
                q, f = g // 4, g % 4
                if g % 16 == 0:
                    wait(eng, a_y, k.count(4, g // 16 - 1))
                if g < 16 and f == 0:
                    wait(eng, g_dc, k.count(4, q + 1))
                wait(eng, a_ev, k.count(64, g + 1))
                for b in range(4):
                    last = mm(yb[g // 16 % 2][b * TS:(b + 1) * TS, f * P:(f + 1) * P], diag_c[:, q % 4, 4 * f + b, :],
                              hT[:, g % 2, b * P:(b + 1) * P], start=g % 16 == 0, stop=q % 4 == 3,
                              skip_group_check=True)
                last.then_inc(p_y, 1)

            def product(bank, pairs, done):
                for i, (lhsT, rhs) in enumerate(pairs):
                    last = mm(bank, lhsT, rhs, start=i == 0, stop=i == len(pairs) - 1)
                last.then_inc(done, 1)

            def in_xi(k, cb, tail_before):
                if cb == 0:
                    wait(eng, l_xt[k.parity], k.row * 16 + (k.half // 2 + 1) * 16)
                if cb < 2 and tail_before:
                    wait(eng, v_r2, k.count(4, -9 - 2 * cb))
                elif cb < 2:
                    wait(eng, v_xb, k.count(4, 0))
                else:
                    wait(eng, a_xi, k.count(8, 2 * cb - 2))
                product(xi_bank(cb)[:, :], [(w_in[:, d, cb * P:(cb + 1) * P], xt[:, k.parity, d, :])
                                            for d in range(DH)], p_xi)

            def in_z(k, cb, head):
                if cb < 2 and head:
                    wait(eng, a_xi, (k + 1).count(8, 2 * cb + 6))
                elif cb < 2:
                    wait(eng, v_r2, k.count(4, -5 - 2 * cb))
                else:
                    wait(eng, a_z, k.count(4, cb - 1))
                product(z_bank(cb)[:, :], [(w_in[:, d, DI + cb * P:DI + (cb + 1) * P], xt[:, k.parity, d, :])
                                           for d in range(DH)], p_z)

            def x_proj(k, z_before):
                wait(eng, a_z, z_before)
                wait(eng, a_xi, k.count(8, 8))
                wait(eng, a_u, k.count(4, 4))
                for c in range(CB):
                    for b in range(2):
                        last = mm(xproj_bank[b * P // 2:b * P // 2 + R + 2 * N, 0:T // 2], w_x[:, c, :],
                                  u[:, k.parity, c, b * T // 2:(b + 1) * T // 2],
                                  start=c == 0, stop=c == CB - 1)
                last.then_inc(p_x, 1)

            def dt_proj(k, cb, z_before):
                if cb == 0:
                    wait(eng, a_z, z_before)
                    wait(eng, a_dbl, k.count(2, 2))
                elif cb > 1:
                    wait(eng, v_xb, k.count(4, cb - 1))
                product(dt_bank(cb)[:, :], [(w_dt[:, cb * P:(cb + 1) * P], dbl[0:R, :])], p_dt)

            def turn_y(k, cb, *before):
                wait(eng, a_y, k.count(4, cb + 1))
                if before:
                    wait(eng, *before)
                for tb in range(TB):
                    last = nc.tensor.transpose(turn_bank(cb)[:, tb * P:(tb + 1) * P],
                                               yt[:, tb * P:(tb + 1) * P], ident[:, :])
                last.then_inc(p_turn, 1)

            def out_proj(k, tb):
                if tb == 0:
                    wait(eng, g_y, k.count(4, 4))
                    wait(eng, v_r2, k.count(4, 0))
                elif tb > 1:
                    wait(eng, v_r1, k.count(4, tb - 1))
                product(out_bank(tb)[:, 0:DM], [(yg[:, c, tb * P:(tb + 1) * P], w_out[:, c, :])
                                                for c in range(CB)], p_out)

            def turn_x1(k, dh):
                wait(eng, v_x1, k.count(4, 4))
                for tb in range(TB):
                    last = nc.tensor.transpose(x1T_bank(dh)[:, tb * P:(tb + 1) * P],
                                               res[:, tb, dh * P:(dh + 1) * P], ident[:, :])
                last.then_inc(p_x1T, 1)

            def gate_up(k, m, weight, bank, done):
                x1 = xt[:, (k.parity + 1) % 2, :, :]
                product(bank[:, :], [(weight[:, d, m * P:(m + 1) * P], x1[:, d, :])
                                     for d in range(DH)], done)

            def gate(k, m, before):
                if m == 0:
                    wait(eng, a_x1T, k.count(2, 2))
                if m < 2:
                    wait(eng, *before)
                else:
                    wait(eng, v_gs, k.count(6, m - 1))
                gate_up(k, m, w_g, gate_bank(m), p_gate)

            def up(k, m, next_chunk):
                if m == 0:
                    wait(eng, a_x1T, k.count(2, 2))
                elif m in (1, 4) and next_chunk:
                    wait(eng, v_y, (k + 1).count(4, m // 4 + 1))
                elif m == 3:
                    wait(eng, v_hid, k.count(6, 3))
                else:
                    wait(eng, v_hid, k.count(6, m - 1))
                gate_up(k, m, w_u, up_bank(m), p_up)

            def down(k, tb, next_chunk):
                if tb == 0:
                    wait(eng, v_hid, k.count(6, 6))
                if tb == 3 and next_chunk:
                    wait(eng, v_y, (k + 1).count(4, 3))
                product(down_bank(tb)[:, 0:DM], [(hid[:, m, tb * P:(tb + 1) * P], w_d[:, m, :])
                                                 for m in range(HB)], p_down)

            def turn(k, cb, tail, first, second):
                if cb == CB - 1:
                    if second:
                        turn_y(k + -1, cb)
                    elif not first:
                        turn_y(k + -1, cb, v_r2, k.count(4, -6))
                elif not tail:
                    turn_y(k, cb, v_y, k.count(4, cb))
                elif cb == 0:
                    turn_y(k, cb, a_x1T, (k + -1).count(2, 1))
                else:
                    turn_y(k, cb, v_hid, (k + -1).count(6, 3 * cb - 1))

            def side(k, q, j, tail, head, first, second):
                for what, i in PE_SIDE.get((q, j), []):
                    if what == "xi" and head:
                        in_xi(k + 1, i, not (first or second))
                    if what == "z":
                        in_z(k, i, head)
                    if what == "xproj" and head:
                        x_proj(k + 1, k.count(4, 4))
                    if what == "dt" and head:
                        dt_proj(k + 1, i, k.count(4, 4))
                    if what == "turn":
                        turn(k, i, tail, first, second)
                    if what == "out" and tail:
                        out_proj(k + -1, i)
                    if what == "x1T" and tail:
                        turn_x1(k + -1, i)
                    if what == "gate" and tail:
                        gate(k + -1, i, (v_xb, (k + 1).count(4, i + 3)) if head else (a_z, k.count(4, 4 - i)))
                    if what == "up" and tail:
                        up(k + -1, i, True)
                    if what == "down" and tail:
                        down(k + -1, i, True)

            def chunk(k, tail, head, first=False, second=False):
                for q in range(QUADS):
                    for j in range(4):
                        g = 4 * (q - 1) + j
                        if g >= 0:
                            transposes(k, g)
                        elif not first:
                            transposes(k + -1, 64 + g)
                        side(k, q, j, tail, head, first, second)
                        if g >= 1:
                            sum_states(k, g - 1)
                        elif not first:
                            sum_states(k + -1, 63 + g)

            eng.wait_ge(l_in, 16)
            k0 = Chunk(0, 0)
            for cb in range(CB):
                in_xi(k0, cb, False)
            eng.wait_ge(l_w, ALL_LOADED)
            x_proj(k0, 0)
            for cb in range(CB):
                dt_proj(k0, cb, 0)
            eng.wait_ge(g_set, 5)
            eng.wait_ge(v_set, SETUP_V)
            for half in range(2):
                chunk(Chunk(0, half), half == 1, True, half == 0, half == 1)
            with eng.Fori(1, ROWS - 1) as row:
                for half in range(2):
                    chunk(Chunk(row, half), True, True)
            for half in range(2):
                chunk(Chunk(ROWS - 1, half), True, half == 0)
            kl = Chunk(ROWS - 1, 1)
            for g in range(60, 64):
                transposes(kl, g)
                sum_states(kl, g - 1)
            sum_states(kl, 63)
            turn_y(kl, CB - 1, v_r2, kl.count(4, -2))
            for tb in range(TB):
                out_proj(kl, tb)
            for dh in range(DH):
                turn_x1(kl, dh)
            for m in range(HB):
                gate(kl, m, (v_r2, kl.count(4, 0)))
                up(kl, m, False)
            for tb in range(TB):
                down(kl, tb, False)


def kernel(L0_attn_x, L0_attn_W_in, L0_attn_conv_w, L0_attn_conv_b, L0_attn_W_xproj, L0_attn_W_dt,
           L0_attn_b_dt, L0_attn_A_log, L0_attn_D_skip, L0_attn_W_out, L0_ffn_w_gate, L0_ffn_w_up,
           L0_ffn_w_down):
    import numpy as np
    import concourse.bacc as bacc
    from concourse.bass_utils import run_bass_kernel_spmd

    def columns(v):
        return np.asarray(v).reshape(-1, P).T

    x = np.ascontiguousarray(L0_attn_x).reshape(-1, DM)
    arrays = {
        "x": x, "xT": x.T, "W_inT": L0_attn_W_in.T, "conv_w": L0_attn_conv_w, "conv_b": columns(L0_attn_conv_b),
        "W_xT": L0_attn_W_xproj.T, "W_dtT": L0_attn_W_dt.T, "b_dt": columns(L0_attn_b_dt), "A_log": L0_attn_A_log,
        "D_skip": columns(L0_attn_D_skip), "W_outT": L0_attn_W_out.T, "w_gT": L0_ffn_w_gate.T,
        "w_uT": L0_ffn_w_up.T, "w_dT": L0_ffn_w_down.T,
    }
    arrays = {f"in_{k}": np.ascontiguousarray(v) for k, v in arrays.items()}
    nc = bacc.Bacc("TRN2", target_bir_lowering=False, num_devices=1)
    args = [nc.dram_tensor(k, v.shape, mybir.dt.from_np(v.dtype), kind="ExternalInput").ap()
            for k, v in arrays.items()]
    out = nc.dram_tensor("out", x.shape, F32, kind="ExternalOutput").ap()
    mamba_ffn(nc, *args, out)
    got = run_bass_kernel_spmd(nc, [arrays], core_ids=[0]).results[0]["out"]
    return got.reshape(L0_attn_x.shape)
```
